# Optimizing a Trainium2 kernel written in Bass

```python
import numpy as np
import jax
import jax.numpy as jnp

def _softmax(x, axis=-1):
    return jax.nn.softmax(x, axis=axis)

def _gelu(x):
    return jax.nn.gelu(x, approximate=True)

def _silu(x):
    return jax.nn.silu(x)

def _sigmoid(x):
    return jax.nn.sigmoid(x)

def _layernorm(x, axis=-1, eps=1e-05):
    m = jnp.mean(x, axis=axis, keepdims=True)
    v = jnp.var(x, axis=axis, keepdims=True)
    return (x - m) / jnp.sqrt(v + eps)

def _scatter_add(tgt, idx, src, axis=0):
    return tgt.at[idx].add(src)

def _segment_sum(src, seg, n):
    return jax.ops.segment_sum(src, seg, n)
kernel_name = 'mk_xattn_ffn_d2_seqx_r8_12bbb5'

def setup_inputs(seed: int=0):
    np.random.seed(seed)
    _w = jnp.asarray

    def _rec_inputs():
        import jax
        import jax.numpy as jnp
        _rk = jax.random.key(seed)
        x = 0.002226 + 0.9996 * jax.random.normal(jax.random.fold_in(_rk, 1), (4, 512, 128), jnp.float32)
        _lenS = 512 - jax.random.randint(jax.random.fold_in(_rk, 7), (4,), 0, max(1, 512 // 4) + 1, jnp.int32)
        _lenS2 = 32 - jax.random.randint(jax.random.fold_in(_rk, 8), (4,), 0, max(1, 32 // 4) + 1, jnp.int32)
        _ctx_1024P = jax.random.normal(jax.random.fold_in(_rk, 11), (4, 16, 128), jnp.float32)
        _ctx_1024c = jax.random.dirichlet(jax.random.fold_in(_rk, 511), 0.3 * jnp.ones((16,), jnp.float32), (4, 32))
        _ctx_1024t = jnp.einsum('bsk,bkd->bsd', _ctx_1024c, _ctx_1024P)
        _ctx_1024t = _ctx_1024t * jax.lax.rsqrt(jnp.mean(jnp.square(_ctx_1024t)) + 1e-12) * 0.953939
        ctx_1024 = -0.000125008 + 0.999885 * (_ctx_1024t + 0.3 * jax.random.normal(jax.random.fold_in(_rk, 611), (4, 32, 128), jnp.float32))
        return (x, ctx_1024)
    x, ctx_1024 = _rec_inputs()

    def _L0_xattn_setup():
        import jax, jax.numpy as jnp
        import numpy as np
        EPS = 1e-05

        def layer_norm(x, g, b):
            mu = jnp.mean(x, axis=-1, keepdims=True)
            var = jnp.var(x, axis=-1, keepdims=True)
            return (x - mu) * jax.lax.rsqrt(var + EPS) * g + b
        key = jax.random.key(seed)
        ks = jax.random.split(key, 8)
        dim, heads, dim_head = (128, 16, 64)
        inner = heads * dim_head
        b, n, m = (8, 512, 64)
        s = dim ** (-0.5)
        return {'x': jax.random.normal(ks[0], (b, n, dim), jnp.float32), 'latents': jax.random.normal(ks[1], (b, m, dim), jnp.float32), 'ln_m_g': jnp.ones((dim,), jnp.float32), 'ln_m_b': jnp.zeros((dim,), jnp.float32), 'ln_l_g': jnp.ones((dim,), jnp.float32), 'ln_l_b': jnp.zeros((dim,), jnp.float32), 'Wq': jax.random.normal(ks[2], (dim, inner), jnp.float32) * s, 'Wkv': jax.random.normal(ks[3], (dim, 2 * inner), jnp.float32) * s, 'Wout': jax.random.normal(ks[4], (inner, dim), jnp.float32) * s}
    _L0_xattn_all = _L0_xattn_setup()
    _L0_xattn_in = {k: v for k, v in _L0_xattn_all.items() if k in ('ln_m_g', 'ln_m_b', 'ln_l_g', 'ln_l_b', 'Wq', 'Wkv', 'Wout')}
    del _L0_xattn_all

    def _L0_ffn_setup():
        import jax, jax.numpy as jnp
        import numpy as np
        B, S, DIM, FFN, E = (4, 256, 128, 512, 8)
        key = jax.random.key(seed)
        k0, k1, k2, k3 = jax.random.split(key, 4)
        scale = 0.02
        return {'hidden_states': jax.random.normal(k0, (B, S, DIM), jnp.float32), 'router_w': jax.random.normal(k1, (DIM, E), jnp.float32) * scale, 'router_b': jnp.zeros((E,), jnp.float32), 'w1': jax.random.normal(k2, (E, DIM, 2 * FFN), jnp.float32) * scale, 'w2': jax.random.normal(k3, (E, FFN, DIM), jnp.float32) * scale}
    _L0_ffn_all = _L0_ffn_setup()
    _L0_ffn_in = {k: v for k, v in _L0_ffn_all.items() if k in ('router_w', 'router_b', 'w1', 'w2')}
    del _L0_ffn_all

    def _L1_xattn_setup():
        import jax, jax.numpy as jnp
        import numpy as np
        D_MODEL = 128
        N_HEAD = 16
        D_HEAD = D_MODEL // N_HEAD
        B, L = (2, 256)
        key = jax.random.key(seed)
        k1, k2, k3, k4, k5 = jax.random.split(key, 5)
        s = 0.02
        return {'q': jax.random.normal(k1, (B, L, D_MODEL), dtype=jnp.float32), 'kv': jax.random.normal(k2, (B, L, D_MODEL), dtype=jnp.float32), 'w_q': jax.random.normal(k3, (D_MODEL, D_MODEL), dtype=jnp.float32) * s, 'w_kv': jax.random.normal(k4, (D_MODEL, 2 * D_HEAD), dtype=jnp.float32) * s, 'w_concat': jax.random.normal(k5, (D_MODEL, D_MODEL), dtype=jnp.float32) * s}
    _L1_xattn_all = _L1_xattn_setup()
    _L1_xattn_in = {k: v for k, v in _L1_xattn_all.items() if k in ('w_q', 'w_kv', 'w_concat')}
    del _L1_xattn_all

    def _L1_ffn_setup():
        import jax, jax.numpy as jnp
        import numpy as np
        from jax import lax
        TOP_K = 2
        key = jax.random.key(seed)
        k0, k1, k2, k3, k4 = jax.random.split(key, 5)
        B, S, H, I, E = (2, 256, 128, 256, 8)
        hidden_states = jax.random.normal(k0, (B, S, H), dtype=jnp.float32)
        Wr = jax.random.normal(k1, (H, E), dtype=jnp.float32) * 0.02
        Wg = jax.random.normal(k2, (E, H, I), dtype=jnp.float32) * 0.02
        Wu = jax.random.normal(k3, (E, H, I), dtype=jnp.float32) * 0.02
        Wd = jax.random.normal(k4, (E, I, H), dtype=jnp.float32) * 0.02
        return {'hidden_states': hidden_states, 'Wr': Wr, 'Wg': Wg, 'Wu': Wu, 'Wd': Wd}
    _L1_ffn_all = _L1_ffn_setup()
    _L1_ffn_in = {k: v for k, v in _L1_ffn_all.items() if k in ('Wr', 'Wg', 'Wu', 'Wd')}
    del _L1_ffn_all
    return {'x': x, 'ctx_1024': ctx_1024, 'L0_xattn_ln_m_g': _L0_xattn_in['ln_m_g'], 'L0_xattn_ln_m_b': _L0_xattn_in['ln_m_b'], 'L0_xattn_ln_l_g': _L0_xattn_in['ln_l_g'], 'L0_xattn_ln_l_b': _L0_xattn_in['ln_l_b'], 'L0_xattn_Wq': _L0_xattn_in['Wq'], 'L0_xattn_Wkv': _L0_xattn_in['Wkv'], 'L0_xattn_Wout': _L0_xattn_in['Wout'], 'L0_ffn_router_w': _L0_ffn_in['router_w'], 'L0_ffn_router_b': _L0_ffn_in['router_b'], 'L0_ffn_w1': _L0_ffn_in['w1'], 'L0_ffn_w2': _L0_ffn_in['w2'], 'L1_xattn_w_q': _L1_xattn_in['w_q'], 'L1_xattn_w_kv': _L1_xattn_in['w_kv'], 'L1_xattn_w_concat': _L1_xattn_in['w_concat'], 'L1_ffn_Wr': _L1_ffn_in['Wr'], 'L1_ffn_Wg': _L1_ffn_in['Wg'], 'L1_ffn_Wu': _L1_ffn_in['Wu'], 'L1_ffn_Wd': _L1_ffn_in['Wd']}

def reference(x, ctx_1024, L0_xattn_ln_m_g, L0_xattn_ln_m_b, L0_xattn_ln_l_g, L0_xattn_ln_l_b, L0_xattn_Wq, L0_xattn_Wkv, L0_xattn_Wout, L0_ffn_router_w, L0_ffn_router_b, L0_ffn_w1, L0_ffn_w2, L1_xattn_w_q, L1_xattn_w_kv, L1_xattn_w_concat, L1_ffn_Wr, L1_ffn_Wg, L1_ffn_Wu, L1_ffn_Wd):
    import jax
    import jax.numpy as jnp

    def _L0_xattn_ref(x, latents, ln_m_g, ln_m_b, ln_l_g, ln_l_b, Wq, Wkv, Wout):
        import jax, jax.numpy as jnp
        import numpy as np
        EPS = 1e-05

        def layer_norm(x, g, b):
            mu = jnp.mean(x, axis=-1, keepdims=True)
            var = jnp.var(x, axis=-1, keepdims=True)
            return (x - mu) * jax.lax.rsqrt(var + EPS) * g + b
        heads, dim_head = (16, 64)
        scale = dim_head ** (-0.5)
        x = layer_norm(x, ln_m_g, ln_m_b)
        lat = layer_norm(latents, ln_l_g, ln_l_b)
        b, m, _ = lat.shape
        q = lat @ Wq
        kv_input = jnp.concatenate([x, lat], axis=1)
        kv = kv_input @ Wkv
        k, v = jnp.split(kv, 2, axis=-1)

        def split_heads(t):
            return t.reshape(t.shape[0], t.shape[1], heads, dim_head).transpose(0, 2, 1, 3)
        q, k, v = (split_heads(q), split_heads(k), split_heads(v))
        dots = jnp.einsum('bhid,bhjd->bhij', q, k) * scale
        attn = jax.nn.softmax(dots, axis=-1)
        out = jnp.einsum('bhij,bhjd->bhid', attn, v)
        out = out.transpose(0, 2, 1, 3).reshape(b, m, heads * dim_head)
        return out @ Wout

    def _L0_ffn_ref(hidden_states, router_w, router_b, w1, w2):
        import jax, jax.numpy as jnp
        import numpy as np
        B, S, DIM, FFN, E = (4, 256, 128, 512, 8)
        b, s, d = hidden_states.shape
        x = hidden_states.reshape(-1, d)
        logits = x @ router_w + router_b
        route = jax.nn.softmax(logits, axis=1)
        max_prob = jnp.max(route, axis=1, keepdims=True)
        max_ind = jnp.argmax(route, axis=1)
        out = jnp.zeros_like(x)
        num_experts = w1.shape[0]
        for e in range(num_experts):
            h = x @ w1[e]
            a, g = jnp.split(h, 2, axis=1)
            y = jax.nn.silu(a) * g @ w2[e]
            out = jnp.where((max_ind == e)[:, None], y, out)
        out = out * max_prob
        return out.reshape(b, s, d)

    def _L1_xattn_ref(q, kv, w_q, w_kv, w_concat):
        import jax, jax.numpy as jnp
        import numpy as np
        D_MODEL = 128
        N_HEAD = 16
        D_HEAD = D_MODEL // N_HEAD
        B, L = (2, 256)
        b, l, d_model = q.shape
        dh = d_model // N_HEAD
        qp = q @ w_q
        kvp = kv @ w_kv
        k, v = (kvp[..., :dh], kvp[..., dh:])
        qh = qp.reshape(b, l, N_HEAD, dh).transpose(0, 2, 1, 3)
        score = jnp.einsum('bhqd,bkd->bhqk', qh, k) / jnp.sqrt(jnp.float32(dh))
        attn = jax.nn.softmax(score, axis=-1)
        out = jnp.einsum('bhqk,bkd->bhqd', attn, v)
        out = out.transpose(0, 2, 1, 3).reshape(b, l, d_model)
        return out @ w_concat

    def _L1_ffn_ref(hidden_states, Wr, Wg, Wu, Wd):
        import jax, jax.numpy as jnp
        import numpy as np
        from jax import lax
        TOP_K = 2
        B, S, H = hidden_states.shape
        x = hidden_states.reshape(B * S, H)
        routes = x @ Wr
        T, E = routes.shape
        top_vals, top_idx = lax.top_k(routes, TOP_K)
        top_w = jax.nn.softmax(top_vals, axis=-1)
        w = jnp.zeros((T, E), dtype=x.dtype).at[jnp.arange(T)[:, None], top_idx].set(top_w)
        gate = jnp.einsum('th,ehi->tei', x, Wg)
        up = jnp.einsum('th,ehi->tei', x, Wu)
        expert_out = jnp.einsum('tei,eih->teh', jax.nn.silu(gate) * up, Wd)
        out = jnp.einsum('te,teh->th', w, expert_out)
        return out.reshape(B, S, H)
    x = x + _L0_xattn_ref(ctx_1024, _layernorm(x, axis=-1), L0_xattn_ln_m_g, L0_xattn_ln_m_b, L0_xattn_ln_l_g, L0_xattn_ln_l_b, L0_xattn_Wq, L0_xattn_Wkv, L0_xattn_Wout)
    x = x + _L0_ffn_ref(_layernorm(x, axis=-1), L0_ffn_router_w, L0_ffn_router_b, L0_ffn_w1, L0_ffn_w2)
    x = x + _L1_xattn_ref(_layernorm(x, axis=-1), ctx_1024, L1_xattn_w_q, L1_xattn_w_kv, L1_xattn_w_concat)
    x = x + _L1_ffn_ref(_layernorm(x, axis=-1), L1_ffn_Wr, L1_ffn_Wg, L1_ffn_Wu, L1_ffn_Wd)
    return x

_drawn_inputs = setup_inputs


def setup_inputs(seed=0):
    import zlib

    import numpy as np

    out = dict(_drawn_inputs(seed))
    spreads = {'L0_xattn_ln_m_g': (1.0, 0.2),
     'L0_xattn_ln_m_b': (0.0, 0.412),
     'L0_xattn_ln_l_g': (1.0, 0.2),
     'L0_xattn_ln_l_b': (0.0, 0.1),
     'L0_ffn_router_b': (0.0, 0.8)}
    factors = {'L0_ffn_router_w': 8.0,
     'L0_ffn_w1': 8.0,
     'L0_ffn_w2': 8.0,
     'L1_xattn_w_q': 64.0,
     'L1_ffn_Wr': 8.0,
     'L1_ffn_Wg': 8.0,
     'L1_ffn_Wu': 8.0,
     'L1_ffn_Wd': 8.0}
    for name, (base, spread) in spreads.items():
        noise = np.random.default_rng([zlib.crc32(name.encode()), seed]).standard_normal(out[name].shape)
        drawn = base * np.exp(spread * noise) if base else spread * noise
        out[name] = jnp.asarray(drawn.astype(out[name].dtype))
    for name, factor in factors.items():
        out[name] = (out[name] * factor).astype(out[name].dtype)
    return out
```

```python
from contextlib import ExitStack

import concourse.bass as bass
from concourse import mybir

F32 = mybir.dt.float32
F32R = mybir.dt.float32r
ALU = mybir.AluOpType
ACT = mybir.ActivationFunctionType
AX = mybir.AxisListType

P = 128
BANK = 512
EPS = 1e-5


class Counter:

    def __init__(self, handle):
        self.handle = handle
        self.value = 0


class Queues:

    def __init__(self):
        self.work = {n: [] for n in ("tensor", "vector", "scalar", "gpsimd", "sync")}
        self.waited = {n: {} for n in self.work}

    def put(self, engine, waits, issue, signal, by=1):
        todo = []
        for mark in waits:
            if mark is None:
                continue
            counter, value = mark
            if self.waited[engine].get(counter, 0) < value:
                self.waited[engine][counter] = value
                todo.append((counter.handle, value))
        signal.value += by
        self.work[engine].append((todo, issue, signal.handle, by))
        return signal, signal.value

    def wait(self, engine, waits):
        self.work[engine].append(([(c.handle, v) for c, v in waits], None, None, 0))

    def emit(self, engine, eng):
        for todo, issue, handle, by in self.work[engine]:
            for h, v in todo:
                eng.wait_ge(h, v)
            if issue is not None:
                issue(eng).then_inc(handle, by)


def build(nc, x, ctx, lnm_g, lnm_b, lnl_g, lnl_b, Wq, Wkv, Wout, rw, rb, w1, w2, cq, ckv, cc, Wr, Wg, Wu, Wd, out):
    B, S, D = x.shape
    M = ctx.shape[1]
    INNER = Wq.shape[1]
    DH = 64
    H = INNER // DH
    E = rw.shape[1]
    F_B = w2.shape[1]
    F_D = Wd.shape[1]
    HC = 16
    DC = D // HC
    TPB = S // P
    NT = B * TPB
    KT = S // P
    KEYS = S + M
    HALF = KEYS // 2
    PAIRS = H // 2
    assert D == P and B * M == P and S == BANK and HC * M == BANK

    with ExitStack() as stack:
        def sb(name, *shape, dt=F32):
            return stack.enter_context(nc.sbuf_tensor(name, [P, *shape], dt))

        def counter(name):
            return Counter(stack.enter_context(nc.semaphore(name)))

        q = Queues()

        X = sb("X", NT, D)
        NRM = sb("NRM", TPB, D)
        CTX = sb("CTX", D)
        CTXN = sb("CTXN", D)
        STATS = sb("STATS", TPB, 6)
        MV = sb("MV", TPB, 2)
        RSTD = sb("RSTD", TPB)
        MINUS_HALF = sb("MINUS_HALF", TPB)
        IDENT = sb("IDENT", P)
        ONES = sb("ONES", P)
        GAINS = sb("GAINS", 4)
        XT = sb("XT", 2, KEYS)
        XTH = sb("XTH", 2, KEYS, dt=F32R)
        XTL = sb("XTL", 2, KEYS, dt=F32R)
        CT = sb("CT", P)
        CTH = sb("CTH", P, dt=F32R)
        CTL = sb("CTL", P, dt=F32R)
        CTRAW = sb("CTRAW", P)
        WA = sb("WA", 3 * INNER)
        WOUT = sb("WOUT", PAIRS, D)
        WVH = sb("WVH", INNER, dt=F32R)
        WVL = sb("WVL", INNER, dt=F32R)
        MH = sb("MH", H, P, dt=F32R)
        ML = sb("ML", H, P, dt=F32R)
        AH = sb("AH", 2, S, dt=F32R)
        AL = sb("AL", 2, S, dt=F32R)
        V = sb("V", 2, KT, INNER)
        VC = sb("VC", INNER)
        PR = sb("PR", 8, KEYS)
        PT = sb("PT", 4, KT, S)
        PTC = WA[:, 0:4 * S].rearrange("p (a n) -> p a n", a=4)
        NEGM = sb("NEGM", 8)
        ROWSUM = sb("ROWSUM", 8)
        RECIP = sb("RECIP", 8)
        OT = sb("OT", PAIRS, S)
        HT = OT
        SIL = sb("SIL", 3, S)
        RW = sb("RW", 2, E)
        RB = sb("RB", E)
        TIE = sb("TIE", TPB, E)
        ROUT = sb("ROUT", 8, TPB, E)
        RSM = sb("RSM", 8, TPB)
        COEF = sb("COEF", NT, E)
        WC = sb("WC", 4, D)
        CTREP = sb("CTREP", B, 4, M)
        KREP = sb("KREP", P)
        VREP = sb("VREP", B, DC)
        MASK1 = sb("MASK1", HC, M)
        MASK2 = sb("MASK2", 4, HC)
        CSTAT = sb("CSTAT", 4, 3, HC)
        KB = PTC[:, :, :].rearrange("p b (h k) -> p b h k", h=HC)
        VB = PT[:, 3, :, :].rearrange("p b (c n) -> p b c n", c=4)
        PSUM = stack.enter_context(nc.psum_tensor("PSUM", [P, 8, BANK], F32))

        XBH = sb("XBH", B, S, dt=F32R)
        XBL = sb("XBL", B, S, dt=F32R)
        EWH = MH[:, :, :].rearrange("p (s a) n -> p s (a n)", s=2)
        EWL = ML[:, :, :].rearrange("p (s a) n -> p s (a n)", s=2)
        EWR = V[:, 0, 0:2, :]
        EW2 = V[:, 1, 0:2, 0:F_B]

        s_pe = counter("pe_done")
        s_dve = counter("dve_done")
        s_act = counter("act_done")
        s_pool = counter("pool_done")
        loads = {}

        def load(name, dst, src, waits=()):
            c = counter("ld_" + name)
            return q.put("sync", waits, lambda e: e.dma_start(dst, src), c, 16)

        def pe(waits, issue):
            return q.put("tensor", waits, issue, s_pe)

        def dve(waits, issue):
            return q.put("vector", waits, issue, s_dve)

        def act(waits, issue):
            return q.put("scalar", waits, issue, s_act)

        def pool(waits, issue):
            return q.put("gpsimd", waits, issue, s_pool)

        x_v = x.rearrange("b (t p) d -> p (b t) d", p=P)
        out_v = out.rearrange("b (t p) d -> p (b t) d", p=P)
        ld_x = [load(f"x{b}", X[:, b * TPB:(b + 1) * TPB, :], x_v[:, b * TPB:(b + 1) * TPB, :]) for b in range(1)]
        ld_ctx = load("ctx", CTX[:, :], ctx.rearrange("b m d -> (b m) d"))
        ld_g = [load(f"g{i}", GAINS[:, i:i + 1], v.rearrange("(d a) -> d a", a=1))
                for i, v in enumerate((lnl_g, lnl_b, lnm_g, lnm_b))]
        ld_wq = load("wq", WA[:, 0:INNER], Wq)
        ld_wkv = load("wkv", WA[:, INNER:3 * INNER], Wkv)
        ld_x += [load(f"x{b}", X[:, b * TPB:(b + 1) * TPB, :], x_v[:, b * TPB:(b + 1) * TPB, :]) for b in range(1, B)]
        ld_wout = load("wout", WOUT[:, :, :], Wout.rearrange("(c p) n -> p c n", p=P))
        ld_rw = [load("rw", RW[:, 0, :], rw), load("wr", RW[:, 1, :], Wr)]
        ld_rb = load("rb", RB[0:1, :], rb.rearrange("(a e) -> a e", a=1))
        ld_cq = load("cq", WC[:, 0, :], cq)
        ld_cc = load("cc", WC[:, 1, :], cc)
        ld_ckv = load("ckv", WC[:, 2, 0:2 * DC], ckv)

        p0 = pool([], lambda e: e.memset(IDENT[:, :], 0.0))
        p1 = pool([], lambda e: e.memset(MASK1[:, :, :], 1.0))
        p2 = pool([], lambda e: e.memset(MASK2[:, :, :], 1.0))
        p3 = pool([p0], lambda e: e.affine_select(out=IDENT[:, :], in_=IDENT[:, :], compare_op=ALU.not_equal, fill=1.0,
                                                  base=0, pattern=[[-1, P]], channel_multiplier=1))
        ident_ready = p3
        half_ready = pool([], lambda e: e.memset(MINUS_HALF[:, :], -0.5))
        ones_ready = pool([], lambda e: e.memset(ONES[:, :], 1.0))
        for i in range(E):
            tie_ready = pool([], lambda e, i=i: e.memset(TIE[:, :, i:i + 1], float(E - i)))
        p4 = pool([p2], lambda e: e.affine_select(out=MASK1[:, :, :], in_=MASK1[:, :, :], compare_op=ALU.is_ge, fill=0.0,
                                                  base=0, pattern=[[-DC, HC], [0, M]], channel_multiplier=1))
        p5 = pool([p4], lambda e: e.affine_select(out=MASK1[:, :, :], in_=MASK1[:, :, :], compare_op=ALU.is_ge, fill=0.0,
                                                  base=DC - 1, pattern=[[DC, HC], [0, M]], channel_multiplier=-1))
        p6 = pool([p4], lambda e: e.affine_select(out=MASK2[:, :, :], in_=MASK2[:, :, :], compare_op=ALU.is_ge, fill=0.0,
                                                  base=0, pattern=[[P, 4], [-M, HC]], channel_multiplier=1))
        masks_ready = pool([p6], lambda e: e.affine_select(out=MASK2[:, :, :], in_=MASK2[:, :, :], compare_op=ALU.is_ge,
                                                           fill=0.0, base=M - 1, pattern=[[-P, 4], [M, HC]],
                                                           channel_multiplier=-1))

        free = {i: None for i in range(8)}

        def split_from(src, hi, lo, waits):
            a = act(waits, lambda e: e.activation(hi, src, ACT.Copy))
            d = dve([*waits, a], lambda e: e.tensor_tensor(lo, src, hi.bitcast(F32), ALU.subtract))
            return a, d

        def three(e, dst, aH, aL, bH, bL, start=True):
            e.matmul(dst, aH, bH, start=start, stop=False)
            e.matmul(dst, aH, bL, start=False, stop=False)
            return e.matmul(dst, aL, bH, start=False, stop=True)

        def layernorm(src, dst, n, waits, free_dst):
            def stats(e):
                for t in range(n):
                    i = e.bn_stats(STATS[:, t, :], src(t))
                return i

            def aggr(e):
                for t in range(n):
                    i = e.bn_aggr(MV[:, t, :], STATS[:, t, :])
                return i

            def apply(e):
                for t in range(n):
                    i = e.tensor_scalar(dst(t), src(t), MV[:, t, 0:1], RSTD[:, t:t + 1], ALU.subtract, ALU.mult)
                return i
            m = dve(waits, stats)
            m = dve([m], aggr)
            m = dve([m], lambda e: e.tensor_scalar(RSTD[:, 0:n], MV[:, 0:n, 1], EPS, None, ALU.add))
            m = pool([m, half_ready], lambda e: e.tensor_tensor(RSTD[:, 0:n], RSTD[:, 0:n], MINUS_HALF[:, 0:n], ALU.pow))
            return dve([m, *free_dst], apply)

        def tile_of(buf):
            return lambda t: buf[:, t, :]

        nrm_read = [None]

        def transposed(n, src, waits, bank):
            def issue(e):
                for t in range(n):
                    i = e.transpose(PSUM[:, bank, t * P:(t + 1) * P], src(t), IDENT[:, :])
                return i
            return pe([*waits, free[bank], ident_ready], issue)

        m = layernorm(lambda t: CTX[:, :], lambda t: CTXN[:, :], 1, [ld_ctx], [])
        t1 = transposed(1, lambda t: CTXN[:, :], [m], 7)
        ct = dve([t1, *ld_g], lambda e: e.tensor_scalar(CT[:, :], PSUM[:, 7, 0:P], GAINS[:, 2:3], GAINS[:, 3:4],
                                                        ALU.mult, ALU.add))
        free[7] = ct
        cth, ctl = split_from(CT[:, :], CTH[:, :], CTL[:, :], [ct])
        t2 = transposed(1, lambda t: CTX[:, :], [ld_ctx], 7)
        ctraw = dve([t2], lambda e: e.tensor_copy(CTRAW[:, :], PSUM[:, 7, 0:P]))
        free[7] = ctraw

        wt = []
        WTB = [V[:, 1, 0, :], V[:, 1, 1, :]]
        for w, ld in ((0, ld_wq), (1, ld_wkv)):
            for half in range(2):
                bank = 2 * w + half
                m = transposed(4, lambda t, w=w, half=half: WA[:, w * INNER + (4 * half + t) * P:w * INNER + (4 * half + t + 1) * P],
                               [ld], bank)
                m = act([m], lambda e, w=w, half=half, bank=bank: e.activation(
                    WTB[w][:, half * 512:half * 512 + 512], PSUM[:, bank, :], ACT.Copy))
                free[bank] = m
                wt.append(m)
        m_ready = {}
        for quad in range(H // 4):
            bank = 4 + quad % 2

            def prod(e, quad=quad, bank=bank):
                for j in range(4):
                    h = 8 * (quad // 2) + quad % 2 + 2 * j
                    r = slice(DH * (h % 2), DH * (h % 2) + DH)
                    c = slice((h // 2) * P, (h // 2 + 1) * P)
                    i = e.matmul(PSUM[:, bank, j * P:(j + 1) * P], WTB[0][r, c], WTB[1][r, c], start=True, stop=True)
                return i
            m = pe([*wt, free[bank]], prod)
            hs = slice(8 * (quad // 2) + quad % 2, 8 * (quad // 2) + 8, 2)
            hi, lo = MH[:, hs, :], ML[:, hs, :]
            src = PSUM[:, bank, :].rearrange("p (a b) -> p a b", a=4)
            a = act([m], lambda e, hi=hi, src=src: e.activation(hi, src, ACT.Copy, scale=DH ** -0.5))
            d = dve([a], lambda e, lo=lo, src=src, hi=hi: e.scalar_tensor_tensor(
                out=lo, in0=src, scalar=DH ** -0.5, in1=hi.bitcast(F32), op0=ALU.mult, op1=ALU.subtract))
            free[bank] = d
            m_ready[quad] = (a, d)
        wtb_read = m
        wvh, wvl = split_from(WA[:, 2 * INNER:3 * INNER], WVH[:, :], WVL[:, :], [ld_wkv])

        xt_ready = {}
        xt_free = {}

        def prepare_a(b, bank):
            k = b % 2
            m = layernorm(lambda t: X[:, b * TPB + t, :], tile_of(NRM), TPB, [ld_x[b]], [nrm_read[0]])
            m = layernorm(tile_of(NRM), tile_of(NRM), TPB, [m], [])
            t = transposed(TPB, tile_of(NRM), [m], bank)
            nrm_read[0] = t
            old = xt_free.get(b - 2)
            d = dve([t, old, ct, *ld_g], lambda e: e.tensor_scalar(XT[:, k, 0:S], PSUM[:, bank, :], GAINS[:, 0:1],
                                                                   GAINS[:, 1:2], ALU.mult, ALU.add))
            d2 = dve([old, ct], lambda e: e.tensor_copy(XT[:, k, S:KEYS], CT[:, b * M:(b + 1) * M]))
            free[bank] = d
            xt_ready[b] = split_from(XT[:, k, :], XTH[:, k, :], XTL[:, k, :], [d2, old])

        v_ready = {}
        pv_done = {}

        def values(b, kt, bank2):
            k = b % 2
            cols = slice(kt * P, (kt + 1) * P)

            def issue(e):
                for n in range(2):
                    c = slice(n * BANK, (n + 1) * BANK)
                    i = three(e, PSUM[:, bank2 + n, :], XTH[:, k, cols], XTL[:, k, cols], WVH[:, c], WVL[:, c])
                return i
            m = pe([*xt_ready[b], wvh, wvl, free[bank2], free[bank2 + 1]], issue)
            a = act([m, pv_done.get((b - 2, PAIRS - 1)), wtb_read], lambda e: e.activation(
                V[:, k, kt, :].rearrange("p (a n) -> p a n", a=2), PSUM[:, bank2:bank2 + 2, :], ACT.Copy))
            free[bank2] = free[bank2 + 1] = a
            v_ready[b] = a

        prepare_a(0, 7)

        def vctx(e):
            for n in range(2):
                c = slice(n * BANK, (n + 1) * BANK)
                i = three(e, PSUM[:, n, :], CTH[:, :], CTL[:, :], WVH[:, c], WVL[:, c])
            return i
        m = pe([cth, ctl, wvh, wvl, free[0], free[1]], vctx)
        vc_ready = act([m], lambda e: e.activation(VC[:, :].rearrange("p (a n) -> p a n", a=2), PSUM[:, 0:2, :], ACT.Copy))
        free[0] = free[1] = vc_ready
        for kt in range(KT):
            values(0, kt, 2 if kt % 2 == 0 else 0)

        a_ready = {}
        a_free = {}

        def project(n):
            b, h = divmod(n, H)
            k, j = b % 2, n % 2
            m = pe([*xt_ready[b], *m_ready[2 * (h // 8) + h % 2], free[7]],
                   lambda e: three(e, PSUM[:, 7, :], MH[:, h, :], ML[:, h, :], XTH[:, k, 0:S], XTL[:, k, 0:S]))
            a = act([m, a_free.get(n - 2)], lambda e: e.activation(AH[:, j, :], PSUM[:, 7, :], ACT.Copy))
            d = dve([m, a], lambda e: e.tensor_tensor(AL[:, j, :], PSUM[:, 7, :], AH[:, j, :].bitcast(F32), ALU.subtract))
            free[7] = d
            a_ready[n] = (a, d)

        p_ready = {}
        p_read = {}
        s_bank = {}

        def scores(u):
            n, qt = divmod(u, TPB)
            b, h = divmod(n, H)
            k, j, r = b % 2, n % 2, u % 8
            bank = 2 * (u % 2)
            qs = slice(qt * P, (qt + 1) * P)

            def issue(e):
                for n2 in range(2):
                    ks = slice(n2 * HALF, (n2 + 1) * HALF)
                    i = three(e, PSUM[:, bank + n2, 0:HALF], AH[:, j, qs], AL[:, j, qs], XTH[:, k, ks], XTL[:, k, ks])
                return i
            m = pe([*a_ready[n], free[bank], free[bank + 1]], issue)
            if qt == TPB - 1:
                a_free[n] = m
                xt_free[b] = m
            sc = PSUM[:, bank:bank + 2, 0:HALF]
            d = dve([m], lambda e: e.tensor_reduce(NEGM[:, r:r + 1], sc, AX.XY, ALU.max, negate=True))
            a = act([d, p_read.get(u - 8)], lambda e: e.activation(
                PR[:, r, :].rearrange("p (a n) -> p a n", a=2), sc, ACT.Exp, bias=NEGM[:, r:r + 1],
                accum_out=ROWSUM[:, r:r + 1]))
            free[bank] = free[bank + 1] = a
            d = dve([a], lambda e: e.reciprocal(RECIP[:, r:r + 1], ROWSUM[:, r:r + 1]))
            p_ready[u] = dve([d], lambda e: e.tensor_scalar(PR[:, r, :], PR[:, r, :], RECIP[:, r:r + 1], None, ALU.mult))

        pt_ready = {}

        def turn(u):
            n, qt = divmod(u, TPB)
            b, h = divmod(n, H)
            r, slot = u % 8, n % 4
            bank = 4 + u % 2

            def issue(e):
                for kt in range(KT):
                    i = e.transpose(PSUM[:, bank, kt * P:(kt + 1) * P], PR[:, r, kt * P:(kt + 1) * P], IDENT[:, :])
                return i
            m = pe([p_ready[u], free[bank]], issue)
            p_read[u] = m
            old = pv_done.get(divmod(n // 2 - 2, PAIRS)) if n // 2 >= 2 else None
            a = act([m, old], lambda e: e.activation(PT[:, slot, :, qt * P:(qt + 1) * P],
                                                     PSUM[:, bank, :].rearrange("p (k n) -> p k n", k=KT), ACT.Copy))
            free[bank] = a
            pt_ready[n] = [a]
            if qt == TPB - 1:
                def issue_c(e):
                    for t in range(TPB):
                        i = e.transpose(PSUM[0:M, 7, t * P:(t + 1) * P], PR[:, (n * TPB + t) % 8, S:KEYS], IDENT[:, :])
                    return i
                m = pe([free[7]], issue_c)
                for t in range(TPB):
                    p_read[n * TPB + t] = m
                c = dve([m, old], lambda e: e.tensor_copy(PTC[b * M:(b + 1) * M, slot, :], PSUM[0:M, 7, :]))
                free[7] = c
                pt_ready[n].append(c)

        ot_ready = {}
        ot_free = [None]

        def attend(pair, kt):
            b, pr = divmod(pair, PAIRS)
            k = b % 2

            def issue(e):
                for j in range(2):
                    n = 2 * pair + j
                    h = n % H
                    dst = PSUM[DH * j:DH * j + DH, 6, :]
                    if kt < KT:
                        i = e.matmul(dst, V[:, k, kt, h * DH:(h + 1) * DH], PT[:, n % 4, kt, :], start=kt == 0, stop=False)
                    else:
                        i = e.matmul(dst, VC[b * M:(b + 1) * M, h * DH:(h + 1) * DH], PTC[b * M:(b + 1) * M, n % 4, :],
                                     start=False, stop=True)
                return i
            waits = [*pt_ready[2 * pair], *pt_ready[2 * pair + 1], v_ready[b], vc_ready, free[6]] if kt == 0 else []
            m = pe(waits, issue)
            if kt == KT:
                pv_done[(b, pr)] = m
                free[6] = dve([m, ot_free[0]], lambda e: e.tensor_copy(OT[:, pr, :], PSUM[:, 6, :]))
                ot_ready[pair] = free[6]

        x_ready = {}

        def add_to_x(b, m, bank):
            xb = X[:, b * TPB:(b + 1) * TPB, :]
            d = dve([m, x_ready.get(b)], lambda e: e.tensor_tensor(xb, xb, PSUM[:, bank, :].rearrange("p (t n) -> p t n", t=TPB),
                                                                   ALU.add))
            free[bank] = d
            x_ready[b] = d

        def project_out(b, src, weight, n, waits, bank):
            def issue(e):
                for t in range(TPB):
                    for c in range(n):
                        i = e.matmul(PSUM[:, bank, t * P:(t + 1) * P], src(c)[:, t * P:(t + 1) * P], weight(c),
                                     start=c == 0, stop=c == n - 1)
                return i
            m = pe([*waits, free[bank]], issue)
            add_to_x(b, m, bank)
            return m

        UNITS = B * H * TPB
        LAG = 2
        pending = []
        project(0)
        project(1)
        for u in range(UNITS + LAG):
            if u < UNITS:
                n, qt = divmod(u, TPB)
                b, h = divmod(n, H)
                if qt == 0 and h == 4 and b + 1 < B:
                    prepare_a(b + 1, 7)
                if qt == 0 and h == 0 and b > 0:
                    for kt in range(KT):
                        values(b, kt, 2 * (kt % 2))
                scores(u)
                if qt == TPB - 1 and n + 2 < B * H:
                    project(n + 2)
            if pending:
                attend(*pending.pop(0))
            if u >= LAG:
                turn(u - LAG)
                if (u - LAG) % (2 * TPB) == 2 * TPB - 1:
                    pair = (u - LAG) // (2 * TPB)
                    while pending:
                        attend(*pending.pop(0))
                    if pair and pair % PAIRS == 0:
                        b = pair // PAIRS - 1
                        ot_free[0] = project_out(b, lambda c: OT[:, c, :], lambda c: WOUT[:, c, :], PAIRS,
                                                 [ot_ready[pair - 1], ld_wout], 7)
                    pending = [(pair, kt) for kt in range(KT + 1)]
        while pending:
            attend(*pending.pop(0))
        ot_read = project_out(B - 1, lambda c: OT[:, c, :], lambda c: WOUT[:, c, :], PAIRS,
                              [ot_ready[B * PAIRS - 1], ld_wout], 7)

        xf = XT[:, 0, 0:S]
        xf_read = [xt_free[B - 2], xt_free[B - 1]]

        def normalised(b, bank, waits=()):
            m = layernorm(lambda t: X[:, b * TPB + t, :], tile_of(NRM), TPB, [x_ready[b], *waits], [nrm_read[0]])
            t = transposed(TPB, tile_of(NRM), [m], bank)
            nrm_read[0] = t
            d = dve([t, *xf_read], lambda e: e.tensor_copy(xf, PSUM[:, bank, :]))
            free[bank] = d
            return d

        def first_largest(vals, top, hot, tmp, tmp2, waits):
            m = dve(waits, lambda e: e.tensor_reduce(top, vals, AX.X, ALU.max))
            m = dve([m], lambda e: e.tensor_tensor(tmp, vals, top.unsqueeze(2).broadcast_to([P, TPB, E]), ALU.is_equal))
            m = dve([m, tie_ready], lambda e: e.tensor_tensor(tmp, tmp, TIE[:, :, :], ALU.mult))
            m = dve([m], lambda e: e.tensor_reduce(tmp2, tmp, AX.X, ALU.max))
            return dve([m], lambda e: e.tensor_tensor(hot, tmp, tmp2.unsqueeze(2).broadcast_to([P, TPB, E]), ALU.is_equal))

        coef_ready = {}
        xb_ready = {}
        xb_free = [None]

        def over_e(v):
            return v.unsqueeze(2).broadcast_to([P, TPB, E])

        def route(b, which, bank):
            d = normalised(b, 7)

            def issue(e):
                for t in range(TPB):
                    dst = PSUM[:, bank, t * E:(t + 1) * E]
                    i = e.matmul(dst, xf[:, t * P:(t + 1) * P], RW[:, which, :], start=True, stop=which == 1)
                    if which == 0:
                        i = e.matmul(dst, ONES[0:1, :], RB[0:1, :], start=False, stop=True)
                return i
            m = pe([d, ld_rw[which], ld_rb, ones_ready, free[bank]], issue)
            xb_ready[b] = split_from(xf, XBH[:, b, :], XBL[:, b, :], [d, xb_free[0]])
            xf_read[:] = [m, *xb_ready[b]]
            L, tmp, hot, hot2, L2, ex = (ROUT[:, i] for i in range(6))
            top, top2, tmp2, sm, rc = (RSM[:, i] for i in range(5))
            coef = COEF[:, b * TPB:(b + 1) * TPB, :]
            m = dve([m], lambda e: e.tensor_copy(L, PSUM[:, bank, 0:TPB * E].rearrange("p (t n) -> p t n", t=TPB)))
            free[bank] = m
            m = first_largest(L, top, hot, tmp, tmp2, [m])
            if which == 0:
                m = dve([m], lambda e: e.tensor_tensor(L2, L, over_e(top), ALU.subtract))
                m = act([m], lambda e: e.activation(ex, L2, ACT.Exp))
                m = dve([m], lambda e: e.tensor_reduce(sm, ex, AX.X, ALU.add))
                m = dve([m], lambda e: e.reciprocal(rc, sm))
                m = dve([m, coef_free[0]], lambda e: e.tensor_tensor(coef, hot, over_e(rc), ALU.mult))
            else:
                m = dve([m], lambda e: e.tensor_scalar(tmp, hot, -1.0, 1.0, ALU.mult, ALU.add))
                m = dve([m], lambda e: e.tensor_tensor(L2, L, tmp, ALU.mult))
                m = dve([m], lambda e: e.scalar_tensor_tensor(out=L2, in0=hot, scalar=-3.4e38, in1=L2, op0=ALU.mult,
                                                              op1=ALU.add))
                m = first_largest(L2, top2, hot2, tmp, tmp2, [m])
                m = dve([m], lambda e: e.tensor_tensor(tmp2, top2, top, ALU.subtract))
                m = act([m], lambda e: e.activation(sm, tmp2, ACT.Exp))
                m = dve([m], lambda e: e.tensor_scalar(rc, sm, 1.0, None, ALU.add))
                m = dve([m], lambda e: e.reciprocal(tmp2, rc))
                m = dve([m], lambda e: e.tensor_tensor(rc, sm, tmp2, ALU.mult))
                m = dve([m], lambda e: e.tensor_tensor(hot, hot, over_e(tmp2), ALU.mult))
                m = dve([m], lambda e: e.tensor_tensor(hot2, hot2, over_e(rc), ALU.mult))
                m = dve([m, coef_free[0]], lambda e: e.tensor_tensor(coef, hot, hot2, ALU.add))
            coef_ready[b] = m

        coef_free = [None]
        w_free, w2_free = {}, {}
        h_free = {i: ot_read for i in range(8)}
        rings = {"set": 0, "h": 0, "y": 0}

        def experts(stage, FF, gate_up, down, x_waits):
            NF = FF // P
            SETS = [0, 2, 4]
            YB = [6, 7]
            ldw = {}

            def fetch(e_):
                s = e_ % 2
                old = [*w_free.get(s, []), *w2_free.get(s, [])]
                a = [load(f"{stage}w{e_}_{i}", EWR[:, s, c:c + n], src, [*old, *x_waits])
                     for i, (c, n, src) in enumerate(gate_up(e_))]
                d = load(f"{stage}d{e_}", EW2[:, s, :].rearrange("p (c n) -> p c n", n=P)[:, 0:NF, :], down(e_),
                         [*old, *x_waits])
                ldw[e_] = (a, d)

            def cut(e_):
                s = e_ % 2
                return split_from(EWR[:, s, 0:2 * FF], EWH[:, s, 0:2 * FF], EWL[:, s, 0:2 * FF],
                                  [*ldw[e_][0], *w_free.get(s, [])])

            ready = {}
            later = []

            def second(e_, b, hts):
                s = e_ % 2
                bank = YB[rings["y"] % 2]
                rings["y"] += 1

                def issue(e):
                    for t in range(TPB):
                        for f in range(NF):
                            i = e.matmul(PSUM[:, bank, t * P:(t + 1) * P], HT[:, hts[f][0], t * P:(t + 1) * P],
                                         EW2[:, s, f * P:(f + 1) * P], start=f == 0, stop=f == NF - 1)
                    return i
                m = pe([hts[-1][1], ldw[e_][1], free[bank]], issue)
                for f in range(NF):
                    h_free[hts[f][0]] = m
                w2_free[s] = [m]
                cf = COEF[:, b * TPB:(b + 1) * TPB, e_:e_ + 1].broadcast_to([P, TPB, D])
                y = rings["y"] % 2
                tmp = PR[:, 4 * y:4 * y + 4, 0:D]
                d = dve([m, coef_ready[b]], lambda e: e.tensor_tensor(
                    tmp, PSUM[:, bank, :].rearrange("p (t n) -> p t n", t=TPB), cf, ALU.mult))
                free[bank] = d
                xb = X[:, b * TPB:(b + 1) * TPB, :]
                x_ready[b] = dve([d, x_ready[b]], lambda e: e.tensor_tensor(xb, xb, tmp, ALU.add))
                coef_free[0] = x_ready[b]
                return m

            fetch(0)
            fetch(1)
            ready[0] = cut(0)
            for e_ in range(E):
                s = e_ % 2
                for b in range(B):
                    hts = []
                    for f in range(NF):
                        bank = SETS[rings["set"] % 3]
                        sl = rings["set"] % 3
                        rings["set"] += 1
                        ht = rings["h"] % 8
                        rings["h"] += 1

                        def issue(e, f=f, bank=bank, b=b, s=s):
                            for n in range(2):
                                c = slice(n * FF + f * P, n * FF + (f + 1) * P)
                                i = three(e, PSUM[:, bank + n, :], EWH[:, s, c], EWL[:, s, c], XBH[:, b, :], XBL[:, b, :])
                            return i
                        m = pe([*ready[e_], *xb_ready[b], free[bank], free[bank + 1]], issue)
                        a = act([m, free[bank]], lambda e, bank=bank, sl=sl: e.activation(
                            SIL[:, sl, :], PSUM[:, bank, :], ACT.Silu))
                        d = dve([m, a, h_free.get(ht)], lambda e, bank=bank, sl=sl, ht=ht: e.tensor_tensor(
                            HT[:, ht, :], SIL[:, sl, :], PSUM[:, bank + 1, :], ALU.mult))
                        free[bank] = free[bank + 1] = d
                        hts.append((ht, d))
                        last_gate = m
                        if later and f == NF - 1 - (NF > 2):
                            second(*later.pop(0))
                    later.append((e_, b, hts))
                    if b == 0 and 1 <= e_ < E - 1:
                        fetch(e_ + 1)
                    if b == 1 and e_ + 1 < E:
                        ready[e_ + 1] = cut(e_ + 1)
                w_free[s] = [last_gate, *ready[e_]]
            second(*later.pop(0))
            xb_free[0] = last_gate

        for b in range(B):
            route(b, 0, b % 4)
        w1_v, w2_v = w1, w2
        last_v = pv_done[(B - 1, PAIRS - 1)]
        experts("b", F_B, lambda e_: [(0, 2 * F_B, w1[e_])],
                lambda e_: w2[e_].rearrange("(c p) n -> p c n", p=P), [last_v])

        WKREP = WC[:, 3, :]
        m = dve([ld_ckv], lambda e: e.tensor_copy(WKREP.rearrange("p (h d) -> p h d", h=HC),
                                                  WC[:, 2, 0:DC].unsqueeze(1).broadcast_to([P, HC, DC])))
        m2 = dve([ctraw], lambda e: e.tensor_copy(
            CTREP[:, :, :, :], CTRAW[:, :].rearrange("p (b k) -> p b k", b=B).unsqueeze(2).broadcast_to([P, B, 4, M])))
        mk = pe([m2, free[0]], lambda e: e.matmul(PSUM[:, 0, 0:P], WKREP, CTRAW[:, :], start=True, stop=True))
        kr = dve([mk], lambda e: e.tensor_copy(KREP[:, :], PSUM[:, 0, 0:P]))
        free[0] = kr

        def vrep(e):
            for b in range(B):
                i = e.matmul(PSUM[:, 1, b * DC:(b + 1) * DC], CTREP[:, b, :, :], WC[:, 2, DC:2 * DC], start=True, stop=True)
            return i
        mv = pe([free[1]], vrep)
        vr = dve([mv], lambda e: e.tensor_copy(VREP[:, :, :], PSUM[:, 1, 0:B * DC].rearrange("p (b d) -> p b d", b=B)))
        free[1] = vr
        kb_ready = {}
        for b in range(B):
            dve([kr, masks_ready], lambda e, b=b: e.tensor_tensor(
                KB[:, b, :, :], MASK1[:, :, :], KREP[:, b * M:(b + 1) * M].unsqueeze(1).broadcast_to([P, HC, M]), ALU.mult))
            kb_ready[b] = dve([vr, masks_ready], lambda e, b=b: e.tensor_tensor(
                VB[:, b, :, :].rearrange("p c (h d) -> p (c h) d", h=HC),
                MASK2[:, :, :].rearrange("p c h -> p (c h)").unsqueeze(2).broadcast_to([P, 4 * HC, DC]),
                VREP[:, b, :].unsqueeze(1).broadcast_to([P, 4 * HC, DC]), ALU.mult))

        QT, OC = HT[:, 0:2, :], HT[:, 2:4, :]
        qt_free, oc_free = {}, {}
        pc_free = {}
        ptc_free = {}
        for b in range(B):
            k = b % 2
            d = normalised(b, 7)
            m = pe([d, ld_cq, free[6]], lambda e: e.matmul(PSUM[:, 6, :], WC[:, 0, :], xf, start=True, stop=True))
            xf_read[:] = [m]
            qr = act([m, qt_free.get(b - 2), h_free.get(k)], lambda e, k=k: e.activation(QT[:, k, :], PSUM[:, 6, :], ACT.Copy))
            free[6] = qr
            turned = []
            for t in range(TPB):
                bank = t
                r = (b * TPB + t) % 4
                pc = PT[:, 2, r, :]
                ps = PSUM[:, bank, :].rearrange("p (h k) -> p h k", h=HC)
                pr = pc.rearrange("p (h k) -> p h k", h=HC)
                top, sm, rc = (CSTAT[:, r, i, :] for i in range(3))
                m = pe([qr, kb_ready[b], free[bank]], lambda e, bank=bank, t=t, k=k, b=b: e.matmul(
                    PSUM[:, bank, :], QT[:, k, t * P:(t + 1) * P], KB[:, b, :, :], start=True, stop=True))
                qt_free[b] = m
                d = dve([m], lambda e, ps=ps, top=top: e.tensor_reduce(top, ps, AX.X, ALU.max))
                d = dve([d, pc_free.get(r)], lambda e, ps=ps, pr=pr, top=top: e.tensor_tensor(
                    pr, ps, top.unsqueeze(2).broadcast_to([P, HC, M]), ALU.subtract))
                free[bank] = d
                a = act([d], lambda e, pc=pc: e.activation(pc, pc, ACT.Exp, scale=DC ** -0.5))
                d = dve([a], lambda e, pr=pr, sm=sm: e.tensor_reduce(sm, pr, AX.X, ALU.add))
                d = dve([d], lambda e, sm=sm, rc=rc: e.reciprocal(rc, sm))
                g = pool([d], lambda e, pr=pr, rc=rc: e.tensor_tensor(
                    pr, pr, rc.unsqueeze(2).broadcast_to([P, HC, M]), ALU.mult))
                turned.append((t, r, pc, g))
            for t, r, pc, g in turned:
                bank = 4 + t % 2

                def issue(e, bank=bank, pc=pc):
                    for c in range(4):
                        i = e.transpose(PSUM[:, bank, c * P:(c + 1) * P], pc[:, c * P:(c + 1) * P], IDENT[:, :])
                    return i
                m = pe([g, free[bank]], issue)
                pc_free[r] = m
                a = act([m, ptc_free.get(b - 2)], lambda e, bank=bank, t=t, k=k: e.activation(
                    PT[:, k, :, t * P:(t + 1) * P], PSUM[:, bank, :].rearrange("p (c n) -> p c n", c=4), ACT.Copy))
                free[bank] = a

            def issue(e, b=b, k=k):
                for c in range(4):
                    i = e.matmul(PSUM[:, 6, :], VB[:, b, c, :], PT[:, k, c, :], start=c == 0, stop=c == 3)
                return i
            m = pe([a, free[6]], issue)
            ptc_free[b] = m
            o = dve([m, oc_free.get(b - 2), h_free.get(2 + k)], lambda e, k=k: e.tensor_copy(OC[:, k, :], PSUM[:, 6, :]))
            free[6] = o
            oc_free[b] = project_out(b, lambda c, k=k: OC[:, k, :], lambda c: WC[:, 1, :], 1, [o, ld_cc], 7)
            route(b, 1, 6)
        for k in range(4):
            h_free[k] = oc_free[B - 1]

        experts("d", F_D, lambda e_: [(0, F_D, Wg[e_]), (F_D, F_D, Wu[e_])],
                lambda e_: Wd[e_].rearrange("(c p) n -> p c n", p=P), [])

        s_out = counter("stored")
        for b in range(B):
            stored = q.put("sync", [x_ready[b]], lambda e, b=b: e.dma_start(
                out_v[:, b * TPB:(b + 1) * TPB, :], X[:, b * TPB:(b + 1) * TPB, :]), s_out, 16)
        q.wait("sync", [stored])

        with nc.Block() as block:
            @block.sync
            def _(eng):
                q.emit("sync", eng)

            @block.gpsimd
            def _(eng):
                q.emit("gpsimd", eng)

            @block.scalar
            def _(eng):
                q.emit("scalar", eng)

            @block.vector
            def _(eng):
                q.emit("vector", eng)

            @block.tensor
            def _(eng):
                q.emit("tensor", eng)


_INS = ['x', 'ctx_1024', 'L0_xattn_ln_m_g', 'L0_xattn_ln_m_b', 'L0_xattn_ln_l_g', 'L0_xattn_ln_l_b', 'L0_xattn_Wq',
        'L0_xattn_Wkv', 'L0_xattn_Wout', 'L0_ffn_router_w', 'L0_ffn_router_b', 'L0_ffn_w1', 'L0_ffn_w2', 'L1_xattn_w_q',
        'L1_xattn_w_kv', 'L1_xattn_w_concat', 'L1_ffn_Wr', 'L1_ffn_Wg', 'L1_ffn_Wu', 'L1_ffn_Wd']


def kernel(**inputs):
    import numpy as _np
    import concourse.bacc as _bacc
    from concourse import mybir as _mybir
    from concourse.bass_utils import run_bass_kernel_spmd as _run

    nc = _bacc.Bacc("TRN2", target_bir_lowering=False, num_devices=1)
    arrays, args = {}, []
    for name in _INS:
        a = _np.ascontiguousarray(inputs[name])
        arrays[f"in_{name}"] = a
        args.append(nc.dram_tensor(f"in_{name}", a.shape, _mybir.dt.from_np(a.dtype), kind="ExternalInput").ap())
    shape = _np.shape(inputs["x"])
    args.append(nc.dram_tensor("out_x", shape, _mybir.dt.float32, kind="ExternalOutput").ap())
    build(nc, *args)
    return _run(nc, [arrays], core_ids=[0]).results[0]["out_x"]
```

```python
from contextlib import ExitStack

import concourse.bass as bass
from concourse import mybir

F32 = mybir.dt.float32
F32R = mybir.dt.float32r
ALU = mybir.AluOpType
ACT = mybir.ActivationFunctionType
AX = mybir.AxisListType

P = 128
BANK = 512
EPS = 1e-5


class Counter:

    def __init__(self, handle):
        self.handle = handle
        self.value = 0


class Queues:

    def __init__(self):
        self.work = {n: [] for n in ("tensor", "vector", "scalar", "gpsimd", "sync")}
        self.waited = {n: {} for n in self.work}

    def put(self, engine, waits, issue, signal, by=1):
        todo = []
        for mark in waits:
            if mark is None:
                continue
            counter, value = mark
            if self.waited[engine].get(counter, 0) < value:
                self.waited[engine][counter] = value
                todo.append((counter.handle, value))
        signal.value += by
        self.work[engine].append((todo, issue, signal.handle, by))
        return signal, signal.value

    def wait(self, engine, waits):
        self.work[engine].append(([(c.handle, v) for c, v in waits], None, None, 0))

    def emit(self, engine, eng):
        for todo, issue, handle, by in self.work[engine]:
            for h, v in todo:
                eng.wait_ge(h, v)
            if issue is not None:
                issue(eng).then_inc(handle, by)


def build(nc, x, ctx, lnm_g, lnm_b, lnl_g, lnl_b, Wq, Wkv, Wout, rw, rb, w1, w2, cq, ckv, cc, Wr, Wg, Wu, Wd, out):
    B, S, D = x.shape
    M = ctx.shape[1]
    INNER = Wq.shape[1]
    DH = 64
    H = INNER // DH
    E = rw.shape[1]
    F_B = w2.shape[1]
    F_D = Wd.shape[1]
    HC = 16
    DC = D // HC
    TPB = S // P
    NT = B * TPB
    KT = S // P
    KEYS = S + M
    HALF = KEYS // 2
    PAIRS = H // 2
    assert D == P and B * M == P and S == BANK and HC * M == BANK

    with ExitStack() as stack:
        def sb(name, *shape, dt=F32):
            return stack.enter_context(nc.sbuf_tensor(name, [P, *shape], dt))

        def counter(name):
            return Counter(stack.enter_context(nc.semaphore(name)))

        q = Queues()

        X = sb("X", NT, D)
        NRM = sb("NRM", TPB, D)
        CTX = sb("CTX", D)
        CTXN = sb("CTXN", D)
        STATS = sb("STATS", B, TPB, 6)
        MV = sb("MV", B, TPB, 2)
        RSTD = sb("RSTD", B, TPB)
        MINUS_HALF = sb("MINUS_HALF", TPB)
        IDENT = sb("IDENT", P)
        ONES = sb("ONES", P)
        GAINS = sb("GAINS", 4)
        XT = sb("XT", KEYS)
        XTH = sb("XTH", 2, KEYS, dt=F32R)
        XTL = sb("XTL", 2, KEYS, dt=F32R)
        CT = sb("CT", P)
        CTH = sb("CTH", P, dt=F32R)
        CTL = sb("CTL", P, dt=F32R)
        CTRAW = sb("CTRAW", P)
        WA = sb("WA", 3 * INNER)
        WOUT = sb("WOUT", PAIRS, D)
        WVH = sb("WVH", INNER, dt=F32R)
        WVL = sb("WVL", INNER, dt=F32R)
        MH = sb("MH", H, P, dt=F32R)
        ML = sb("ML", H, P, dt=F32R)
        AH = sb("AH", 2, S, dt=F32R)
        AL = sb("AL", 2, S, dt=F32R)
        V = sb("V", 2, KT, INNER)
        VC = sb("VC", INNER)
        PR = sb("PR", 8, KEYS)
        PT = sb("PT", 4, KT, S)
        PTC = WA[:, 0:4 * S].rearrange("p (a n) -> p a n", a=4)
        NEGM = sb("NEGM", 8)
        ROWSUM = sb("ROWSUM", 8)
        RECIP = sb("RECIP", 8)
        OT = sb("OT", PAIRS, S)
        HT = OT
        SIL = sb("SIL", 3, S)
        RW = sb("RW", 2, E)
        RB = sb("RB", E)
        TIE = sb("TIE", TPB, E)
        ROUT = sb("ROUT", 6, TPB, E)
        RSM = sb("RSM", 8, TPB)
        COEF = sb("COEF", NT, E)
        WC = sb("WC", 4, D)
        CTREP = sb("CTREP", B, 4, M)
        KREP = sb("KREP", P)
        VREP = sb("VREP", B, DC)
        MASK1 = sb("MASK1", HC, M)
        MASK2 = sb("MASK2", 4, HC)
        CSTAT = sb("CSTAT", 4, 3, HC)
        KB = PTC[:, :, :].rearrange("p b (h k) -> p b h k", h=HC)
        VB = PT[:, 3, :, :].rearrange("p b (c n) -> p b c n", c=4)
        PSUM = stack.enter_context(nc.psum_tensor("PSUM", [P, 8, BANK], F32))

        XBH = sb("XBH", B, S, dt=F32R)
        XBL = sb("XBL", B, S, dt=F32R)
        EWH = MH[:, :, :].rearrange("p (s a) n -> p s (a n)", s=2)
        EWL = ML[:, :, :].rearrange("p (s a) n -> p s (a n)", s=2)
        EWR = V[:, 0, 0:2, :]
        EW2 = V[:, 0, 2, :].rearrange("p (s n) -> p s n", s=2)

        s_pe = counter("pe_done")
        s_dve = counter("dve_done")
        s_act = counter("act_done")
        s_pool = counter("pool_done")
        loads = {}

        def load(name, dst, src, waits=()):
            c = counter("ld_" + name)
            return q.put("sync", waits, lambda e: e.dma_start(dst, src), c, 16)

        def pe(waits, issue):
            return q.put("tensor", waits, issue, s_pe)

        def dve(waits, issue):
            return q.put("vector", waits, issue, s_dve)

        def act(waits, issue):
            return q.put("scalar", waits, issue, s_act)

        def pool(waits, issue):
            return q.put("gpsimd", waits, issue, s_pool)

        x_v = x.rearrange("b (t p) d -> p (b t) d", p=P)
        out_v = out.rearrange("b (t p) d -> p (b t) d", p=P)
        ld_x = [load(f"x{b}", X[:, b * TPB:(b + 1) * TPB, :], x_v[:, b * TPB:(b + 1) * TPB, :]) for b in range(1)]
        ld_ctx = load("ctx", CTX[:, :], ctx.rearrange("b m d -> (b m) d"))
        ld_g = [load(f"g{i}", GAINS[:, i:i + 1], v.rearrange("(d a) -> d a", a=1))
                for i, v in enumerate((lnl_g, lnl_b, lnm_g, lnm_b))]
        ld_wq = load("wq", WA[:, 0:INNER], Wq)
        ld_wkv = load("wkv", WA[:, INNER:3 * INNER], Wkv)
        ld_x += [load(f"x{b}", X[:, b * TPB:(b + 1) * TPB, :], x_v[:, b * TPB:(b + 1) * TPB, :]) for b in range(1, B)]
        ld_wout = load("wout", WOUT[:, :, :], Wout.rearrange("(c p) n -> p c n", p=P))
        ld_rw = [load("rw", RW[:, 0, :], rw), load("wr", RW[:, 1, :], Wr)]
        ld_rb = load("rb", RB[0:1, :], rb.rearrange("(a e) -> a e", a=1))
        ld_cq = load("cq", WC[:, 0, :], cq)
        ld_cc = load("cc", WC[:, 1, :], cc)
        ld_ckv = load("ckv", WC[:, 2, 0:2 * DC], ckv)

        p0 = pool([], lambda e: e.memset(IDENT[:, :], 0.0))
        p1 = pool([], lambda e: e.memset(MASK1[:, :, :], 1.0))
        p2 = pool([], lambda e: e.memset(MASK2[:, :, :], 1.0))
        p3 = pool([p0], lambda e: e.affine_select(out=IDENT[:, :], in_=IDENT[:, :], compare_op=ALU.not_equal, fill=1.0,
                                                  base=0, pattern=[[-1, P]], channel_multiplier=1))
        ident_ready = p3
        half_ready = pool([], lambda e: e.memset(MINUS_HALF[:, :], -0.5))
        ones_ready = pool([], lambda e: e.memset(ONES[:, :], 1.0))
        for i in range(E):
            tie_ready = pool([], lambda e, i=i: e.memset(TIE[:, :, i:i + 1], float(E - i)))
        p4 = pool([p2], lambda e: e.affine_select(out=MASK1[:, :, :], in_=MASK1[:, :, :], compare_op=ALU.is_ge, fill=0.0,
                                                  base=0, pattern=[[-DC, HC], [0, M]], channel_multiplier=1))
        p5 = pool([p4], lambda e: e.affine_select(out=MASK1[:, :, :], in_=MASK1[:, :, :], compare_op=ALU.is_ge, fill=0.0,
                                                  base=DC - 1, pattern=[[DC, HC], [0, M]], channel_multiplier=-1))
        p6 = pool([p4], lambda e: e.affine_select(out=MASK2[:, :, :], in_=MASK2[:, :, :], compare_op=ALU.is_ge, fill=0.0,
                                                  base=0, pattern=[[P, 4], [-M, HC]], channel_multiplier=1))
        masks_ready = pool([p6], lambda e: e.affine_select(out=MASK2[:, :, :], in_=MASK2[:, :, :], compare_op=ALU.is_ge,
                                                           fill=0.0, base=M - 1, pattern=[[-P, 4], [M, HC]],
                                                           channel_multiplier=-1))

        free = {i: None for i in range(8)}

        def split_from(src, hi, lo, waits):
            a = act(waits, lambda e: e.activation(hi, src, ACT.Copy))
            d = dve([*waits, a], lambda e: e.tensor_tensor(lo, src, hi.bitcast(F32), ALU.subtract))
            return a, d

        def three(e, dst, aH, aL, bH, bL, start=True):
            e.matmul(dst, aH, bH, start=start, stop=False)
            e.matmul(dst, aH, bL, start=False, stop=False)
            return e.matmul(dst, aL, bH, start=False, stop=True)

        def layernorm(src, dst, n, j, waits, free_dst):
            def stats(e):
                for t in range(n):
                    i = e.bn_stats(STATS[:, j, t, :], src(t))
                return i

            def aggr(e):
                for t in range(n):
                    i = e.bn_aggr(MV[:, j, t, :], STATS[:, j, t, :])
                return i

            def apply(e):
                for t in range(n):
                    i = e.tensor_scalar(dst(t), src(t), MV[:, j, t, 0:1], RSTD[:, j, t:t + 1], ALU.subtract, ALU.mult)
                return i
            rstd = RSTD[:, j, 0:n]
            m = dve(waits, stats)
            yield
            m = dve([m], aggr)
            m = dve([m], lambda e: e.tensor_scalar(rstd, MV[:, j, 0:n, 1], EPS, None, ALU.add))
            m = pool([m, half_ready], lambda e: e.tensor_tensor(rstd, rstd, MINUS_HALF[:, 0:n], ALU.pow))
            yield
            m = dve([m, *free_dst], apply)
            yield
            return m

        def finish(gen):
            try:
                while True:
                    next(gen)
            except StopIteration as stop:
                return stop.value

        background = []

        def advance(steps=1, lanes=1):
            for _ in range(steps):
                for gen in background[:lanes]:
                    try:
                        next(gen)
                    except StopIteration:
                        background.remove(gen)

        def tile_of(buf):
            return lambda t: buf[:, t, :]

        nrm_read = {}

        def transposed(n, src, waits, bank):
            def issue(e):
                for t in range(n):
                    i = e.transpose(PSUM[:, bank, t * P:(t + 1) * P], src(t), IDENT[:, :])
                return i
            return pe([*waits, free[bank], ident_ready], issue)

        m = finish(layernorm(lambda t: CTX[:, :], lambda t: CTXN[:, :], 1, 1, [ld_ctx], []))
        t1 = transposed(1, lambda t: CTXN[:, :], [m], 7)
        ct = dve([t1, *ld_g], lambda e: e.tensor_scalar(CT[:, :], PSUM[:, 7, 0:P], GAINS[:, 2:3], GAINS[:, 3:4],
                                                        ALU.mult, ALU.add))
        free[7] = ct
        cth, ctl = split_from(CT[:, :], CTH[:, :], CTL[:, :], [ct])
        t2 = transposed(1, lambda t: CTX[:, :], [ld_ctx], 7)
        ctraw = dve([t2], lambda e: e.tensor_copy(CTRAW[:, :], PSUM[:, 7, 0:P]))
        free[7] = ctraw

        wt = []
        WTB = [V[:, 1, 0, :], V[:, 1, 1, :]]
        for w, ld in ((0, ld_wq), (1, ld_wkv)):
            for half in range(2):
                bank = 2 * w + half
                m = transposed(4, lambda t, w=w, half=half: WA[:, w * INNER + (4 * half + t) * P:w * INNER + (4 * half + t + 1) * P],
                               [ld], bank)
                m = act([m], lambda e, w=w, half=half, bank=bank: e.activation(
                    WTB[w][:, half * 512:half * 512 + 512], PSUM[:, bank, :], ACT.Copy))
                free[bank] = m
                wt.append(m)
        m_ready = {}
        for quad in range(H // 4):
            bank = 4 + quad % 2

            def prod(e, quad=quad, bank=bank):
                for j in range(4):
                    h = 8 * (quad // 2) + quad % 2 + 2 * j
                    r = slice(DH * (h % 2), DH * (h % 2) + DH)
                    c = slice((h // 2) * P, (h // 2 + 1) * P)
                    i = e.matmul(PSUM[:, bank, j * P:(j + 1) * P], WTB[0][r, c], WTB[1][r, c], start=True, stop=True)
                return i
            m = pe([*wt, free[bank]], prod)
            hs = slice(8 * (quad // 2) + quad % 2, 8 * (quad // 2) + 8, 2)
            hi, lo = MH[:, hs, :], ML[:, hs, :]
            src = PSUM[:, bank, :].rearrange("p (a b) -> p a b", a=4)
            a = act([m], lambda e, hi=hi, src=src: e.activation(hi, src, ACT.Copy, scale=DH ** -0.5))
            d = dve([a], lambda e, lo=lo, src=src, hi=hi: e.scalar_tensor_tensor(
                out=lo, in0=src, scalar=DH ** -0.5, in1=hi.bitcast(F32), op0=ALU.mult, op1=ALU.subtract))
            free[bank] = d
            m_ready[quad] = (a, d)
        wtb_read = m
        wvh, wvl = split_from(WA[:, 2 * INNER:3 * INNER], WVH[:, :], WVL[:, :], [ld_wkv])

        xt_ready = {}
        xth_free = {}
        xt_read = []

        def prepare_a(b, bank):
            k = b % 2
            m = yield from layernorm(lambda t: X[:, b * TPB + t, :], tile_of(NRM), TPB, 0, [ld_x[b]], [nrm_read.get(0)])
            m = yield from layernorm(tile_of(NRM), tile_of(NRM), TPB, 0, [m], [])
            t = transposed(TPB, tile_of(NRM), [m], bank)
            nrm_read[0] = t
            d = dve([t, *xt_read, ct, *ld_g], lambda e: e.tensor_scalar(XT[:, 0:S], PSUM[:, bank, :], GAINS[:, 0:1],
                                                                        GAINS[:, 1:2], ALU.mult, ALU.add))
            d2 = dve([], lambda e: e.tensor_copy(XT[:, S:KEYS], CT[:, b * M:(b + 1) * M]))
            free[bank] = d
            yield
            xt_ready[b] = split_from(XT[:, :], XTH[:, k, :], XTL[:, k, :], [d2, xth_free.get(b - 2)])
            xt_read[:] = xt_ready[b]

        v_ready = {}
        pv_done = {}

        sets = [0]

        def next_set():
            sets[0] += 1
            return 2 * (sets[0] % 2)

        def values(b, kt):
            bank2 = next_set()
            k = b % 2
            cols = slice(kt * P, (kt + 1) * P)

            def issue(e):
                for n in range(2):
                    c = slice(n * BANK, (n + 1) * BANK)
                    i = three(e, PSUM[:, bank2 + n, :], XTH[:, k, cols], XTL[:, k, cols], WVH[:, c], WVL[:, c])
                return i
            m = pe([*xt_ready[b], wvh, wvl, free[bank2], free[bank2 + 1]], issue)
            a = act([m, pv_done.get((b - 2, PAIRS - 1)), wtb_read], lambda e: e.activation(
                V[:, k, kt, :].rearrange("p (a n) -> p a n", a=2), PSUM[:, bank2:bank2 + 2, :], ACT.Copy))
            free[bank2] = free[bank2 + 1] = a
            v_ready[b] = a

        finish(prepare_a(0, 7))

        def vctx(e):
            for n in range(2):
                c = slice(n * BANK, (n + 1) * BANK)
                i = three(e, PSUM[:, n, :], CTH[:, :], CTL[:, :], WVH[:, c], WVL[:, c])
            return i
        m = pe([cth, ctl, wvh, wvl, free[0], free[1]], vctx)
        vc_ready = act([m], lambda e: e.activation(VC[:, :].rearrange("p (a n) -> p a n", a=2), PSUM[:, 0:2, :], ACT.Copy))
        free[0] = free[1] = vc_ready
        for kt in range(KT):
            values(0, kt)

        a_ready = {}
        a_free = {}
        project_done = [None]

        def project(n):
            b, h = divmod(n, H)
            k, j = b % 2, n % 2
            m = pe([*xt_ready[b], *m_ready[2 * (h // 8) + h % 2], free[7]],
                   lambda e: three(e, PSUM[:, 7, :], MH[:, h, :], ML[:, h, :], XTH[:, k, 0:S], XTL[:, k, 0:S]))
            a = act([m, a_free.get(n - 2)], lambda e: e.activation(AH[:, j, :], PSUM[:, 7, :], ACT.Copy))
            d = dve([m, a], lambda e: e.tensor_tensor(AL[:, j, :], PSUM[:, 7, :], AH[:, j, :].bitcast(F32), ALU.subtract))
            free[7] = d
            a_ready[n] = (a, d)
            project_done[0] = m

        p_ready = {}
        p_read = {}
        exp_done = {}

        def scores(u):
            n, qt = divmod(u, TPB)
            b, h = divmod(n, H)
            k, j, r = b % 2, n % 2, u % 8
            bank = next_set()
            qs = slice(qt * P, (qt + 1) * P)

            def issue(e):
                for n2 in range(2):
                    ks = slice(n2 * HALF, (n2 + 1) * HALF)
                    i = three(e, PSUM[:, bank + n2, 0:HALF], AH[:, j, qs], AL[:, j, qs], XTH[:, k, ks], XTL[:, k, ks])
                return i
            m = pe([*a_ready[n], free[bank], free[bank + 1]], issue)
            if qt == TPB - 1:
                a_free[n] = m
                xth_free[b] = m
            sc = PSUM[:, bank:bank + 2, 0:HALF]
            d = dve([m], lambda e: e.tensor_reduce(NEGM[:, r:r + 1], sc, AX.XY, ALU.max, negate=True))
            a = act([d, p_read.get(u - 8)], lambda e: e.activation(
                PR[:, r, :].rearrange("p (a n) -> p a n", a=2), sc, ACT.Exp, bias=NEGM[:, r:r + 1],
                accum_out=ROWSUM[:, r:r + 1]))
            free[bank] = free[bank + 1] = exp_done[u] = a

        def normalise(u):
            r = u % 8
            d = dve([exp_done[u]], lambda e: e.reciprocal(RECIP[:, r:r + 1], ROWSUM[:, r:r + 1]))
            p_ready[u] = dve([d], lambda e: e.tensor_scalar(PR[:, r, :], PR[:, r, :], RECIP[:, r:r + 1], None, ALU.mult))

        pt_ready = {}

        def turn(u):
            n, qt = divmod(u, TPB)
            b, h = divmod(n, H)
            r, slot = u % 8, n % 4
            bank = 4 + u % 2

            def issue(e):
                for kt in range(KT):
                    i = e.transpose(PSUM[:, bank, kt * P:(kt + 1) * P], PR[:, r, kt * P:(kt + 1) * P], IDENT[:, :])
                return i
            m = pe([p_ready[u], free[bank]], issue)
            p_read[u] = m
            old = pv_done.get(divmod(n // 2 - 2, PAIRS)) if n // 2 >= 2 else None
            a = act([m, old], lambda e: e.activation(PT[:, slot, :, qt * P:(qt + 1) * P],
                                                     PSUM[:, bank, :].rearrange("p (k n) -> p k n", k=KT), ACT.Copy))
            free[bank] = a
            pt_ready[n] = [a]
            if qt == TPB - 1:
                def issue_c(e):
                    for t in range(TPB):
                        i = e.transpose(PSUM[0:M, 7, t * P:(t + 1) * P], PR[:, (n * TPB + t) % 8, S:KEYS], IDENT[:, :])
                    return i
                m = pe([free[7]], issue_c)
                for t in range(TPB):
                    p_read[n * TPB + t] = m
                c = dve([m, old], lambda e: e.tensor_copy(PTC[b * M:(b + 1) * M, slot, :], PSUM[0:M, 7, :]))
                free[7] = c
                pt_ready[n].append(c)

        ot_ready = {}
        ot_free = [None]

        def attend(pair, kt):
            b, pr = divmod(pair, PAIRS)
            k = b % 2

            def issue(e):
                for j in range(2):
                    n = 2 * pair + j
                    h = n % H
                    dst = PSUM[DH * j:DH * j + DH, 6, :]
                    if kt < KT:
                        i = e.matmul(dst, V[:, k, kt, h * DH:(h + 1) * DH], PT[:, n % 4, kt, :], start=kt == 0, stop=False)
                    else:
                        i = e.matmul(dst, VC[b * M:(b + 1) * M, h * DH:(h + 1) * DH], PTC[b * M:(b + 1) * M, n % 4, :],
                                     start=False, stop=True)
                return i
            waits = [*pt_ready[2 * pair], *pt_ready[2 * pair + 1], v_ready[b], vc_ready, free[6]] if kt == 0 else []
            m = pe(waits, issue)
            if kt == KT:
                pv_done[(b, pr)] = m
                free[6] = dve([m, ot_free[0]], lambda e: e.tensor_copy(OT[:, pr, :], PSUM[:, 6, :]))
                ot_ready[pair] = free[6]

        x_ready = {}

        def add_to_x(b, m, bank):
            xb = X[:, b * TPB:(b + 1) * TPB, :]
            d = dve([m, x_ready.get(b)], lambda e: e.tensor_tensor(xb, xb, PSUM[:, bank, :].rearrange("p (t n) -> p t n", t=TPB),
                                                                   ALU.add))
            free[bank] = d
            x_ready[b] = d

        def project_out(b, src, weight, n, waits, bank):
            def issue(e):
                for t in range(TPB):
                    for c in range(n):
                        i = e.matmul(PSUM[:, bank, t * P:(t + 1) * P], src(c)[:, t * P:(t + 1) * P], weight(c),
                                     start=c == 0, stop=c == n - 1)
                return i
            m = pe([*waits, free[bank]], issue)
            add_to_x(b, m, bank)
            return m

        coef_free = [None]
        xf = XT[:, 0:S]

        def normalised(b, nrm, xf, key, bank):
            m = yield from layernorm(lambda t: X[:, b * TPB + t, :], nrm, TPB, key % 4, [x_ready[b]], [nrm_read.get(key)])
            t = transposed(TPB, nrm, [m], bank)
            nrm_read[key] = t
            d = dve([t, *xf_read.get(key, [])], lambda e: e.tensor_copy(xf, PSUM[:, bank, :]))
            free[bank] = d
            yield
            return d

        def first_largest(vals, top, hot, tmp, tmp2, waits):
            m = dve(waits, lambda e: e.tensor_reduce(top, vals, AX.X, ALU.max))
            m = dve([m], lambda e: e.tensor_tensor(tmp, vals, top.unsqueeze(2).broadcast_to([P, TPB, E]), ALU.is_equal))
            yield
            m = dve([m, tie_ready], lambda e: e.tensor_tensor(tmp, tmp, TIE[:, :, :], ALU.mult))
            m = dve([m], lambda e: e.tensor_reduce(tmp2, tmp, AX.X, ALU.max))
            m = dve([m], lambda e: e.tensor_tensor(hot, tmp, tmp2.unsqueeze(2).broadcast_to([P, TPB, E]), ALU.is_equal))
            yield
            return m

        coef_ready = {}
        routed = set()
        xb_ready = {}
        xb_free = [None]
        xf_read = {0: xt_read}

        def over_e(v):
            return v.unsqueeze(2).broadcast_to([P, TPB, E])

        def route(b, which, bank, nrm, xf, key):
            d = yield from normalised(b, nrm, xf, key, bank)

            def issue(e):
                for t in range(TPB):
                    dst = PSUM[:, bank, t * E:(t + 1) * E]
                    i = e.matmul(dst, xf[:, t * P:(t + 1) * P], RW[:, which, :], start=True, stop=which == 1)
                    if which == 0:
                        i = e.matmul(dst, ONES[0:1, :], RB[0:1, :], start=False, stop=True)
                return i
            m = pe([d, ld_rw[which], ld_rb, ones_ready, free[bank]], issue)
            L, tmp, hot, hot2, L2, ex = (ROUT[:, i] for i in range(6))
            top, top2, tmp2, sm, rc = (RSM[:, i] for i in range(5))
            coef = COEF[:, b * TPB:(b + 1) * TPB, :]
            lg = dve([m], lambda e: e.tensor_copy(L, PSUM[:, bank, 0:TPB * E].rearrange("p (t n) -> p t n", t=TPB)))
            free[bank] = lg
            xb_ready[b] = split_from(xf, XBH[:, b, :], XBL[:, b, :], [d, xb_free[0]])
            xf_read[key][:] = [m, *xb_ready[b]]
            yield
            m = yield from first_largest(L, top, hot, tmp, tmp2, [lg])
            if which == 0:
                m = dve([m], lambda e: e.tensor_tensor(L2, L, over_e(top), ALU.subtract))
                m = act([m], lambda e: e.activation(ex, L2, ACT.Exp))
                yield
                m = dve([m], lambda e: e.tensor_reduce(sm, ex, AX.X, ALU.add))
                m = dve([m], lambda e: e.reciprocal(rc, sm))
                m = dve([m, coef_free[0]], lambda e: e.tensor_tensor(coef, hot, over_e(rc), ALU.mult))
            else:
                m = dve([m], lambda e: e.tensor_scalar(tmp, hot, -1.0, 1.0, ALU.mult, ALU.add))
                m = dve([m], lambda e: e.tensor_tensor(L2, L, tmp, ALU.mult))
                m = dve([m], lambda e: e.scalar_tensor_tensor(out=L2, in0=hot, scalar=-3.4e38, in1=L2, op0=ALU.mult,
                                                              op1=ALU.add))
                m = yield from first_largest(L2, top2, hot2, tmp, tmp2, [m])
                m = dve([m], lambda e: e.tensor_tensor(tmp2, top2, top, ALU.subtract))
                m = act([m], lambda e: e.activation(sm, tmp2, ACT.Exp))
                yield
                m = dve([m], lambda e: e.tensor_scalar(rc, sm, 1.0, None, ALU.add))
                m = dve([m], lambda e: e.reciprocal(tmp2, rc))
                m = dve([m], lambda e: e.tensor_tensor(rc, sm, tmp2, ALU.mult))
                m = dve([m], lambda e: e.tensor_tensor(hot, hot, over_e(tmp2), ALU.mult))
                m = dve([], lambda e: e.tensor_tensor(hot2, hot2, over_e(rc), ALU.mult))
                m = dve([m, coef_free[0]], lambda e: e.tensor_tensor(coef, hot, hot2, ALU.add))
            coef_ready[b] = m
            routed.add(b)

        UNITS = B * H * TPB
        LAG = 3
        pending = []

        def values_of(b):
            for kt in range(KT):
                values(b, kt)
                yield

        def out_of(b):
            ot_free[0] = project_out(b, lambda c: OT[:, c, :], lambda c: WOUT[:, c, :], PAIRS,
                                     [ot_ready[(b + 1) * PAIRS - 1], ld_wout], 7)

        project(0)
        project(1)
        for u in range(UNITS + LAG):
            if u < UNITS:
                n, qt = divmod(u, TPB)
                b, h = divmod(n, H)
                if qt == 0 and h == 3:
                    if b > 0:
                        background.append(route(b - 1, 0, 7, tile_of(NRM), xf, 0))
                    if b + 1 < B:
                        background.append(prepare_a(b + 1, 7))
                        background.append(values_of(b + 1))
                scores(u)
                if qt == TPB - 1 and n + 2 < B * H:
                    project(n + 2)
            if 1 <= u <= UNITS:
                normalise(u - 1)
            if pending:
                attend(*pending.pop(0))
            advance()
            if u >= LAG:
                turn(u - LAG)
                if (u - LAG) % (2 * TPB) == 2 * TPB - 1:
                    pair = (u - LAG) // (2 * TPB)
                    while pending:
                        attend(*pending.pop(0))
                    if pair and pair % PAIRS == 0:
                        out_of(pair // PAIRS - 1)
                    pending = [(pair, kt) for kt in range(KT + 1)]

        w_free, w2_free = {}, {}
        h_free = {}
        rings = {"set": 0, "h": 0, "y": 0}
        norm_buf = [V[:, 1, b, 0:S].rearrange("p (t n) -> p t n", t=TPB) for b in range(B)]
        feat_buf = [V[:, 1, b, S:2 * S] for b in range(B)]

        def experts(stage, FF, gate_up, down, waits, after):
            NF = FF // P
            SETS = [0, 2, 4]
            YB = [6, 7]
            ldw = {}

            def fetch(e_):
                s = e_ % 2
                old = [*waits, *w_free.get(s, []), *w2_free.get(s, [])]
                a = [load(f"{stage}w{e_}_{i}", EWR[:, s, c:c + n], src, old) for i, (c, n, src) in enumerate(gate_up(e_))]
                d = load(f"{stage}d{e_}", EW2[:, s, :].rearrange("p (c n) -> p c n", n=P)[:, 0:NF, :], down(e_), old)
                ldw[e_] = (a, d)

            def cut(e_):
                s = e_ % 2
                return split_from(EWR[:, s, 0:2 * FF], EWH[:, s, 0:2 * FF], EWL[:, s, 0:2 * FF],
                                  [*ldw[e_][0], *w_free.get(s, [])])

            ready = {}
            later = []

            def second(e_, b, hts):
                s = e_ % 2
                bank = YB[rings["y"] % 2]
                rings["y"] += 1

                def issue(e):
                    for t in range(TPB):
                        for f in range(NF):
                            i = e.matmul(PSUM[:, bank, t * P:(t + 1) * P], HT[:, hts[f][0], t * P:(t + 1) * P],
                                         EW2[:, s, f * P:(f + 1) * P], start=f == 0, stop=f == NF - 1)
                    return i
                m = pe([hts[-1][1], ldw[e_][1], free[bank]], issue)
                for f in range(NF):
                    h_free[hts[f][0]] = m
                w2_free[s] = [m]
                cf = COEF[:, b * TPB:(b + 1) * TPB, e_:e_ + 1].broadcast_to([P, TPB, D])
                y = rings["y"] % 2
                tmp = PR[:, 4 * y:4 * y + 4, 0:D]
                d = dve([m, coef_ready[b]], lambda e: e.tensor_tensor(
                    tmp, PSUM[:, bank, :].rearrange("p (t n) -> p t n", t=TPB), cf, ALU.mult))
                free[bank] = d
                xb = X[:, b * TPB:(b + 1) * TPB, :]
                x_ready[b] = dve([d, x_ready[b]], lambda e: e.tensor_tensor(xb, xb, tmp, ALU.add))
                coef_free[0] = x_ready[b]
                return m

            fetch(0)
            fetch(1)
            ready[0] = cut(0)

            def run():
                for e_ in range(E):
                    s = e_ % 2
                    for b in range(B):
                        while b not in routed:
                            advance()
                        hts = []
                        for f in range(NF):
                            sl = rings["set"] % 3
                            bank = SETS[sl]
                            rings["set"] += 1
                            ht = rings["h"] % 8
                            rings["h"] += 1

                            def issue(e, f=f, bank=bank, b=b, s=s):
                                for n in range(2):
                                    c = slice(n * FF + f * P, n * FF + (f + 1) * P)
                                    i = three(e, PSUM[:, bank + n, :], EWH[:, s, c], EWL[:, s, c], XBH[:, b, :], XBL[:, b, :])
                                return i
                            m = pe([*ready[e_], *xb_ready[b], free[bank], free[bank + 1]], issue)
                            a = act([m, free[bank]], lambda e, bank=bank, sl=sl: e.activation(
                                SIL[:, sl, :], PSUM[:, bank, :], ACT.Silu))
                            d = dve([m, a, h_free.get(ht)], lambda e, bank=bank, sl=sl, ht=ht: e.tensor_tensor(
                                HT[:, ht, :], SIL[:, sl, :], PSUM[:, bank + 1, :], ALU.mult))
                            free[bank] = free[bank + 1] = d
                            hts.append((ht, d))
                            last_gate = m
                            if later and f == NF - 1 - (NF > 2):
                                last = later.pop(0)
                                second(*last)
                                if last[0] == E - 1:
                                    after(last[1])
                            advance(2 if NF == 2 else 1)
                        later.append((e_, b, hts))
                        if b == 0 and 1 <= e_ < E - 1:
                            fetch(e_ + 1)
                        if b == 1 and e_ + 1 < E:
                            ready[e_ + 1] = cut(e_ + 1)
                    w_free[s] = [last_gate, *ready[e_]]
                last = later.pop(0)
                second(*last)
                after(last[1])
                xb_free[0] = last_gate
            return run

        run_b = experts("b", F_B, lambda e_: [(0, 2 * F_B, w1[e_])], lambda e_: w2[e_].rearrange("(c p) n -> p c n", p=P),
                        [pv_done[(B - 2, PAIRS - 1)], project_done[0]], lambda b: background.append(prepare_c(b)))
        while pending:
            attend(*pending.pop(0))
        out_of(B - 1)
        for i in range(8):
            h_free[i] = ot_free[0]
        background.append(route(B - 1, 0, 7, tile_of(NRM), xf, 0))

        QT = [V[:, 1, b, 0:S] for b in range(B)]
        OC = HT[:, 4:6, :]
        q_ready, q_read, oc_free, pc_free, ptc_free = {}, {}, {}, {}, {}

        def prepare_c(b):
            d = yield from normalised(b, tile_of(norm_buf[b]), feat_buf[b], b + 4, 7)
            m = pe([d, ld_cq, free[7]], lambda e: e.matmul(PSUM[:, 7, :], WC[:, 0, :], feat_buf[b], start=True, stop=True))
            xf_read[b + 4] = [m]
            q_ready[b] = act([m], lambda e: e.activation(QT[b], PSUM[:, 7, :], ACT.Copy))
            free[7] = q_ready[b]
            yield

        def h_all():
            return [h_free.get(i) for i in range(8)]

        run_b()

        run_d = experts("d", F_D, lambda e_: [(0, F_D, Wg[e_]), (F_D, F_D, Wu[e_])],
                        lambda e_: Wd[e_].rearrange("(c p) n -> p c n", p=P), [], lambda b: None)
        WKREP = WC[:, 3, :]
        m = dve([ld_ckv], lambda e: e.tensor_copy(WKREP.rearrange("p (h d) -> p h d", h=HC),
                                                  WC[:, 2, 0:DC].unsqueeze(1).broadcast_to([P, HC, DC])))
        m2 = dve([ctraw], lambda e: e.tensor_copy(
            CTREP[:, :, :, :], CTRAW[:, :].rearrange("p (b k) -> p b k", b=B).unsqueeze(2).broadcast_to([P, B, 4, M])))
        mk = pe([m2, free[0]], lambda e: e.matmul(PSUM[:, 0, 0:P], WKREP, CTRAW[:, :], start=True, stop=True))
        kr = dve([mk], lambda e: e.tensor_copy(KREP[:, :], PSUM[:, 0, 0:P]))
        free[0] = kr

        def vrep(e):
            for b in range(B):
                i = e.matmul(PSUM[:, 1, b * DC:(b + 1) * DC], CTREP[:, b, :, :], WC[:, 2, DC:2 * DC], start=True, stop=True)
            return i
        mv = pe([free[1]], vrep)
        vr = dve([mv], lambda e: e.tensor_copy(VREP[:, :, :], PSUM[:, 1, 0:B * DC].rearrange("p (b d) -> p b d", b=B)))
        free[1] = vr
        kb_ready, vb_ready = {}, {}
        for b in range(B):
            kb_ready[b] = pool([kr, masks_ready], lambda e, b=b: e.tensor_tensor(
                KB[:, b, :, :], MASK1[:, :, :], KREP[:, b * M:(b + 1) * M].unsqueeze(1).broadcast_to([P, HC, M]), ALU.mult))
            vb_ready[b] = pool([vr, masks_ready], lambda e, b=b: e.tensor_tensor(
                VB[:, b, :, :].rearrange("p c (h d) -> p (c h) d", h=HC),
                MASK2[:, :, :].rearrange("p c h -> p (c h)").unsqueeze(2).broadcast_to([P, 4 * HC, DC]),
                VREP[:, b, :].unsqueeze(1).broadcast_to([P, 4 * HC, DC]), ALU.mult))

        def over_k(v):
            return v.unsqueeze(2).broadcast_to([P, HC, M])

        def heads_of(v):
            return v.rearrange("p (h k) -> p h k", h=HC)

        c_exp, c_norm, c_turned = {}, {}, {}

        def scores_c(i):
            b, t = divmod(i, TPB)
            bank, r = i % 4, i % 4
            m = pe([q_ready[b], kb_ready[b], free[bank]], lambda e: e.matmul(
                PSUM[:, bank, :], QT[b][:, t * P:(t + 1) * P], KB[:, b, :, :], start=True, stop=True))
            q_read[b] = m
            top, pc = CSTAT[:, r, 0, :], PT[:, 2, r, :]
            d = dve([m], lambda e: e.tensor_reduce(top, heads_of(PSUM[:, bank, :]), AX.X, ALU.max))
            d = dve([d, pc_free.get(r)], lambda e: e.tensor_tensor(heads_of(pc), heads_of(PSUM[:, bank, :]), over_k(top),
                                                                   ALU.subtract))
            free[bank] = d
            c_exp[i] = act([d], lambda e: e.activation(pc, pc, ACT.Exp, scale=DC ** -0.5))

        def normalise_c(i):
            r = i % 4
            sm, rc, pc = CSTAT[:, r, 1, :], CSTAT[:, r, 2, :], PT[:, 2, r, :]
            d = dve([c_exp[i]], lambda e: e.tensor_reduce(sm, heads_of(pc), AX.X, ALU.add))
            d = dve([d], lambda e: e.reciprocal(rc, sm))
            c_norm[i] = pool([d], lambda e: e.tensor_tensor(heads_of(pc), heads_of(pc), over_k(rc), ALU.mult))

        def turn_c(i):
            b, t = divmod(i, TPB)
            k, r, bank = b % 2, i % 4, 4 + i % 2
            pc = PT[:, 2, r, :]

            def issue(e):
                for c in range(4):
                    j = e.transpose(PSUM[:, bank, c * P:(c + 1) * P], pc[:, c * P:(c + 1) * P], IDENT[:, :])
                return j
            m = pe([c_norm[i], free[bank]], issue)
            pc_free[r] = m
            a = act([m, ptc_free.get(b - 2)], lambda e: e.activation(
                PT[:, k, :, t * P:(t + 1) * P], PSUM[:, bank, :].rearrange("p (c n) -> p c n", c=4), ACT.Copy))
            free[bank] = a
            c_turned[b] = a

        def out_c(b):
            k = b % 2

            def issue(e):
                for c in range(4):
                    i = e.matmul(PSUM[:, 6, :], VB[:, b, c, :], PT[:, k, c, :], start=c == 0, stop=c == 3)
                return i
            m = pe([c_turned[b], vb_ready[b], free[6]], issue)
            ptc_free[b] = m
            o = dve([m, oc_free.get(b - 2), *h_all()], lambda e: e.tensor_copy(OC[:, k, :], PSUM[:, 6, :]))
            free[6] = o
            yield
            oc_free[b] = project_out(b, lambda c: OC[:, k, :], lambda c: WC[:, 1, :], 1, [o, ld_cc], 6)
            yield
            yield from route(b, 1, 7, tile_of(norm_buf[b]), feat_buf[b], b + 4)

        LAG_C = 2
        routed.clear()
        while background:
            advance(1, 4)
        for i in range(NT + LAG_C):
            if i < NT:
                scores_c(i)
            if 1 <= i <= NT:
                normalise_c(i - 1)
            advance(3)
            if i >= LAG_C:
                turn_c(i - LAG_C)
                if (i - LAG_C) % TPB == TPB - 1:
                    background.append(out_c((i - LAG_C) // TPB))
        while oc_free.get(B - 1) is None:
            advance()
        for i in (4, 5):
            h_free[i] = oc_free[B - 1]

        run_d()

        s_out = counter("stored")
        for b in range(B):
            stored = q.put("sync", [x_ready[b]], lambda e, b=b: e.dma_start(
                out_v[:, b * TPB:(b + 1) * TPB, :], X[:, b * TPB:(b + 1) * TPB, :]), s_out, 16)
        q.wait("sync", [stored])

        with nc.Block() as block:
            @block.sync
            def _(eng):
                q.emit("sync", eng)

            @block.gpsimd
            def _(eng):
                q.emit("gpsimd", eng)

            @block.scalar
            def _(eng):
                q.emit("scalar", eng)

            @block.vector
            def _(eng):
                q.emit("vector", eng)

            @block.tensor
            def _(eng):
                q.emit("tensor", eng)


_INS = ['x', 'ctx_1024', 'L0_xattn_ln_m_g', 'L0_xattn_ln_m_b', 'L0_xattn_ln_l_g', 'L0_xattn_ln_l_b', 'L0_xattn_Wq',
        'L0_xattn_Wkv', 'L0_xattn_Wout', 'L0_ffn_router_w', 'L0_ffn_router_b', 'L0_ffn_w1', 'L0_ffn_w2', 'L1_xattn_w_q',
        'L1_xattn_w_kv', 'L1_xattn_w_concat', 'L1_ffn_Wr', 'L1_ffn_Wg', 'L1_ffn_Wu', 'L1_ffn_Wd']


def kernel(**inputs):
    import numpy as _np
    import concourse.bacc as _bacc
    from concourse import mybir as _mybir
    from concourse.bass_utils import run_bass_kernel_spmd as _run

    nc = _bacc.Bacc("TRN2", target_bir_lowering=False, num_devices=1)
    arrays, args = {}, []
    for name in _INS:
        a = _np.ascontiguousarray(inputs[name])
        arrays[f"in_{name}"] = a
        args.append(nc.dram_tensor(f"in_{name}", a.shape, _mybir.dt.from_np(a.dtype), kind="ExternalInput").ap())
    shape = _np.shape(inputs["x"])
    args.append(nc.dram_tensor("out_x", shape, _mybir.dt.float32, kind="ExternalOutput").ap())
    build(nc, *args)
    return _run(nc, [arrays], core_ids=[0]).results[0]["out_x"]
```

```python
from contextlib import ExitStack

import concourse.bass as bass
from concourse import mybir

F32 = mybir.dt.float32
F32R = mybir.dt.float32r
I32 = mybir.dt.int32
U32 = mybir.dt.uint32
ALU = mybir.AluOpType
ACT = mybir.ActivationFunctionType
AX = mybir.AxisListType

P = 128
BANK = 512
EPS = 1e-5


class Counter:

    def __init__(self, handle):
        self.handle = handle
        self.value = 0


class Queues:

    def __init__(self):
        self.work = {n: [] for n in ("tensor", "vector", "scalar", "gpsimd", "sync")}
        self.waited = {n: {} for n in self.work}

    def put(self, engine, waits, issue, signal, by=1):
        todo = []
        for mark in waits:
            if mark is None:
                continue
            counter, value = mark
            if self.waited[engine].get(counter, 0) < value:
                self.waited[engine][counter] = value
                todo.append((counter.handle, value))
        signal.value += by
        self.work[engine].append((todo, issue, signal.handle, by))
        return signal, signal.value

    def wait(self, engine, waits):
        self.work[engine].append(([(c.handle, v) for c, v in waits], None, None, 0))

    def emit(self, engine, eng):
        for todo, issue, handle, by in self.work[engine]:
            for h, v in todo:
                eng.wait_ge(h, v)
            if issue is not None:
                issue(eng).then_inc(handle, by)


def build(nc, x, ctx, lnm_g, lnm_b, lnl_g, lnl_b, Wq, Wkv, Wout, rw, rb, w1, w2, cq, ckv, cc, Wr, Wg, Wu, Wd, out):
    B, S, D = x.shape
    M = ctx.shape[1]
    INNER = Wq.shape[1]
    DH = 64
    H = INNER // DH
    E = rw.shape[1]
    F_B = w2.shape[1]
    F_D = Wd.shape[1]
    HC = 16
    DC = D // HC
    TPB = S // P
    NT = B * TPB
    KT = S // P
    KEYS = S + M
    HALF = KEYS // 2
    PAIRS = H // 2
    N = B * S
    ROW = D + 2
    TILES_B = (N - E) // P + E
    TILES_D = (2 * N - E) // P + E
    assert D == P and B * M == P and S == BANK and HC * M == BANK

    with ExitStack() as stack:
        def sb(name, *shape, dt=F32):
            return stack.enter_context(nc.sbuf_tensor(name, [P, *shape], dt))

        def counter(name):
            return Counter(stack.enter_context(nc.semaphore(name)))

        q = Queues()

        X = sb("X", NT, D)
        NRM = sb("NRM", TPB, ROW)
        CTX = sb("CTX", D)
        CTXN = sb("CTXN", D)
        STATS = sb("STATS", B, TPB, 6)
        MV = sb("MV", B, TPB, 2)
        RSTD = sb("RSTD", B, TPB)
        MINUS_HALF = sb("MINUS_HALF", TPB)
        IDENT = sb("IDENT", P)
        ONES = sb("ONES", P)
        GAINS = sb("GAINS", 4)
        XT = sb("XT", KEYS)
        XTH = sb("XTH", 2, KEYS, dt=F32R)
        XTL = sb("XTL", 2, KEYS, dt=F32R)
        CT = sb("CT", P)
        CTH = sb("CTH", P, dt=F32R)
        CTL = sb("CTL", P, dt=F32R)
        CTRAW = sb("CTRAW", P)
        WA = sb("WA", 3 * INNER)
        WOUT = sb("WOUT", PAIRS, D)
        WVH = sb("WVH", INNER, dt=F32R)
        WVL = sb("WVL", INNER, dt=F32R)
        MH = sb("MH", H, P, dt=F32R)
        ML = sb("ML", H, P, dt=F32R)
        AH = sb("AH", 2, S, dt=F32R)
        AL = sb("AL", 2, S, dt=F32R)
        BIG = sb("BIG", 3, KT * INNER)
        V = BIG[:, 1:3, :].rearrange("p k (t n) -> p k t n", t=KT)
        VC = sb("VC", INNER)
        PR = sb("PR", 8, KEYS)
        PT = sb("PT", 4, KT, S)
        PTC = WA[:, 0:4 * S].rearrange("p (a n) -> p a n", a=4)
        NEGM = sb("NEGM", 8)
        ROWSUM = sb("ROWSUM", 8)
        RECIP = sb("RECIP", 8)
        OT = sb("OT", PAIRS, S)
        SIL = sb("SIL", 3, S)
        RW = sb("RW", 2, E)
        RB = sb("RB", E)
        TIE = sb("TIE", TPB, E)
        ROUT = sb("ROUT", 2, 6, TPB, E)
        RSM = sb("RSM", 2, 7, TPB)
        FILL = sb("FILL", TPB)
        PLACE = sb("PLACE", 2, 2, TPB, E)
        SLOT = sb("SLOT", 2, 2, TPB, dt=I32)
        RUN = sb("RUN", 2, NT + 1, E)
        LOWER = sb("LOWER", P)
        JP = sb("JP", TILES_D)
        EMPTY = sb("EMPTY", ROW)
        LIN = sb("LIN", E * NT)
        INCL = sb("INCL", E, E)
        TAB = sb("TAB", 4, E)
        ROW_OF = sb("ROW_OF", TILES_D, dt=I32)
        W_OF = sb("W_OF", TILES_D, dt=I32)
        W2_OF = sb("W2_OF", TILES_D, dt=I32)
        IDX = sb("IDX", 8, dt=I32)
        HAS = sb("HAS", E, NT)
        TAB8 = sb("TAB8", E, E)
        LINROW = sb("LINROW", 2, TILES_D)
        DUMP = sb("DUMP", TILES_D)
        WC = sb("WC", 4, D)
        KREP = sb("KREP", P)
        VREP = sb("VREP", B, DC)
        CSTAT = sb("CSTAT", 4, 3, HC)
        MASK1 = PT[:, 0, 0, :].rearrange("p (h k) -> p h k", h=HC)
        MASK2 = PT[:, 0, 1, 0:4 * HC].rearrange("p (c h) -> p c h", c=4)
        CTREP = PT[:, 0, 2, :].rearrange("p (b c k) -> p b c k", b=B, c=4)
        KB = PTC[:, :, :].rearrange("p b (h k) -> p b h k", h=HC)
        VB = PT[:, 3, :, :].rearrange("p b (c n) -> p b c n", c=4)
        PSUM = stack.enter_context(nc.psum_tensor("PSUM", [P, 8, BANK], F32))

        W1ALL = BIG[:, 0:2, :].rearrange("p a n -> p (a n)")
        W2ALL = BIG[:, 2, :]
        WGUALL = BIG[:, 0, :]
        WDALL = BIG[:, 1, 0:E * 2 * F_D]
        RINGS = PT[:, 1, :, :].rearrange("p k n -> p (k n)")
        XG = RINGS[:, 0:8 * ROW].rearrange("p (r n) -> p r n", n=ROW)
        XGT = RINGS[:, 8 * ROW:8 * ROW + 3 * P].rearrange("p (r n) -> p r n", n=P)
        YS = RINGS[:, 8 * ROW + 3 * P:8 * ROW + 7 * P].rearrange("p (r n) -> p r n", n=P)
        HIDT = OT[:, 6:8, :]
        PASSED = SIL[:, 0, 0:TILES_D * E].rearrange("p (j e) -> p j e", e=E)
        SHIFT = SIL[:, 1, 0:TILES_D * E].rearrange("p (j e) -> p j e", e=E)

        INTS = SIL[:, 2, 0:E * NT].bitcast(I32)

        def dram(name, rows, width):
            return nc.dram_tensor(name, [rows, width], F32, kind="Internal").ap()
        LIST = [dram("lists_b", E * N + TILES_B * P, ROW), dram("lists_d", E * N + TILES_D * P, ROW)]
        RES = [dram("results_b", N + TILES_B * P, D), dram("results_d", 2 * N + TILES_D * P, D)]

        s_pe = counter("pe_done")
        s_dve = counter("dve_done")
        s_act = counter("act_done")
        s_pool = counter("pool_done")
        loads = {}

        def load(name, dst, src, waits=()):
            c = counter("ld_" + name)
            return q.put("sync", waits, lambda e: e.dma_start(dst, src), c, 16)

        def pe(waits, issue):
            return q.put("tensor", waits, issue, s_pe)

        def dve(waits, issue):
            return q.put("vector", waits, issue, s_dve)

        def act(waits, issue):
            return q.put("scalar", waits, issue, s_act)

        def pool(waits, issue):
            return q.put("gpsimd", waits, issue, s_pool)

        x_v = x.rearrange("b (t p) d -> p (b t) d", p=P)
        out_v = out.rearrange("b (t p) d -> p (b t) d", p=P)
        ld_x = [load(f"x{b}", X[:, b * TPB:(b + 1) * TPB, :], x_v[:, b * TPB:(b + 1) * TPB, :]) for b in range(1)]
        ld_ctx = load("ctx", CTX[:, :], ctx.rearrange("b m d -> (b m) d"))
        ld_g = [load(f"g{i}", GAINS[:, i:i + 1], v.rearrange("(d a) -> d a", a=1))
                for i, v in enumerate((lnl_g, lnl_b, lnm_g, lnm_b))]
        ld_wq = load("wq", WA[:, 0:INNER], Wq)
        ld_wkv = load("wkv", WA[:, INNER:3 * INNER], Wkv)
        ld_x += [load(f"x{b}", X[:, b * TPB:(b + 1) * TPB, :], x_v[:, b * TPB:(b + 1) * TPB, :]) for b in range(1, B)]
        ld_wout = load("wout", WOUT[:, :, :], Wout.rearrange("(c p) n -> p c n", p=P))
        ld_rw = [load("rw", RW[:, 0, :], rw), load("wr", RW[:, 1, :], Wr)]
        ld_rb = load("rb", RB[0:1, :], rb.rearrange("(a e) -> a e", a=1))
        ld_cq = load("cq", WC[:, 0, :], cq)
        ld_cc = load("cc", WC[:, 1, :], cc)
        ld_ckv = load("ckv", WC[:, 2, 0:2 * DC], ckv)

        empty = [pool([], lambda e: e.memset(EMPTY[:, :], 0.0))]
        empty = [pool(empty, lambda e: e.memset(EMPTY[:, D:D + 1], -1.0))]

        def clear(which):
            c = counter(f"cleared_{which}")
            rows = LIST[which].shape[0]
            view = LIST[which].rearrange("(p n) w -> p n w", p=P)
            n = rows // P
            for i in range(4):
                a, z = i * n // 4, (i + 1) * n // 4
                m = q.put("sync", empty, lambda e, a=a, z=z: e.dma_start(
                    view[:, a:z, :], EMPTY[:, :].unsqueeze(1).broadcast_to([P, z - a, ROW])), c, 16)
            return m
        cleared = [clear(0), clear(1)]
        ld_w1 = [load("w1a", W1ALL[:, 0:4 * 2 * F_B].rearrange("p (e n) -> p e n", e=4), w1[0:4].rearrange("e p n -> p e n"))]

        p0 = pool([], lambda e: e.memset(IDENT[:, :], 0.0))
        p3 = pool([p0], lambda e: e.affine_select(out=IDENT[:, :], in_=IDENT[:, :], compare_op=ALU.not_equal, fill=1.0,
                                                  base=0, pattern=[[-1, P]], channel_multiplier=1))
        ident_ready = p3
        half_ready = pool([], lambda e: e.memset(MINUS_HALF[:, :], -0.5))
        ones_ready = pool([], lambda e: e.memset(ONES[:, :], 1.0))
        for i in range(E):
            tie_ready = pool([], lambda e, i=i: e.memset(TIE[:, :, i:i + 1], float(E - i)))
        lower_ready = pool([ones_ready], lambda e: e.affine_select(
            out=LOWER[:, :], in_=ONES[:, :], compare_op=ALU.is_gt, fill=0.0, base=0, pattern=[[1, P]], channel_multiplier=-1))
        m = pool([], lambda e: e.iota(INTS[:, 0:TILES_D], [[P, TILES_D]], base=0, channel_multiplier=1))
        jp_ready = dve([m], lambda e: e.tensor_copy(JP[:, :], INTS[:, 0:TILES_D]))
        m = pool([jp_ready], lambda e: e.iota(INTS[:, :], [[P, E * NT]], base=0, channel_multiplier=0))
        lin_ready = dve([m], lambda e: e.tensor_copy(LIN[:, :], INTS[:, :]))
        m = pool([], lambda e: e.memset(INCL[:, :, :], 1.0))
        incl_ready = pool([m], lambda e: e.affine_select(out=INCL[:, :, :], in_=INCL[:, :, :], compare_op=ALU.is_ge, fill=0.0,
                                                         base=0, pattern=[[1, E], [-1, E]], channel_multiplier=0))
        for which in range(2):
            for i in range(E):
                run_ready = pool([], lambda e, i=i, which=which: e.memset(RUN[:, which, 0, i:i + 1], float(i * N)))

        free = {i: None for i in range(8)}

        def split_from(src, hi, lo, waits):
            a = act(waits, lambda e: e.activation(hi, src, ACT.Copy))
            d = dve([*waits, a], lambda e: e.tensor_tensor(lo, src, hi.bitcast(F32), ALU.subtract))
            return a, d

        def three(e, dst, aH, aL, bH, bL, start=True):
            e.matmul(dst, aH, bH, start=start, stop=False)
            e.matmul(dst, aH, bL, start=False, stop=False)
            return e.matmul(dst, aL, bH, start=False, stop=True)

        def layernorm(src, dst, n, j, waits, free_dst):
            def stats(e):
                for t in range(n):
                    i = e.bn_stats(STATS[:, j, t, :], src(t))
                return i

            def aggr(e):
                for t in range(n):
                    i = e.bn_aggr(MV[:, j, t, :], STATS[:, j, t, :])
                return i

            def apply(e):
                for t in range(n):
                    i = e.tensor_scalar(dst(t), src(t), MV[:, j, t, 0:1], RSTD[:, j, t:t + 1], ALU.subtract, ALU.mult)
                return i
            rstd = RSTD[:, j, 0:n]
            m = dve(waits, stats)
            yield
            m = dve([m], aggr)
            m = dve([m], lambda e: e.tensor_scalar(rstd, MV[:, j, 0:n, 1], EPS, None, ALU.add))
            m = pool([m, half_ready], lambda e: e.tensor_tensor(rstd, rstd, MINUS_HALF[:, 0:n], ALU.pow))
            yield
            m = dve([m, *free_dst], apply)
            yield
            return m

        def finish(gen):
            try:
                while True:
                    next(gen)
            except StopIteration as stop:
                return stop.value

        background = []

        def advance(steps=1, lanes=1):
            for _ in range(steps):
                for gen in background[:lanes]:
                    try:
                        next(gen)
                    except StopIteration:
                        background.remove(gen)

        def tile_of(buf):
            return lambda t: buf[:, t, 0:D]

        rows_read = {}
        normed = {}
        nrm_read = {}

        def transposed(n, src, waits, bank):
            def issue(e):
                for t in range(n):
                    i = e.transpose(PSUM[:, bank, t * P:(t + 1) * P], src(t), IDENT[:, :])
                return i
            return pe([*waits, free[bank], ident_ready], issue)

        m = finish(layernorm(lambda t: CTX[:, :], lambda t: CTXN[:, :], 1, 1, [ld_ctx], []))
        t1 = transposed(1, lambda t: CTXN[:, :], [m], 7)
        ct = dve([t1, *ld_g], lambda e: e.tensor_scalar(CT[:, :], PSUM[:, 7, 0:P], GAINS[:, 2:3], GAINS[:, 3:4],
                                                        ALU.mult, ALU.add))
        free[7] = ct
        cth, ctl = split_from(CT[:, :], CTH[:, :], CTL[:, :], [ct])
        t2 = transposed(1, lambda t: CTX[:, :], [ld_ctx], 7)
        ctraw = dve([t2], lambda e: e.tensor_copy(CTRAW[:, :], PSUM[:, 7, 0:P]))
        free[7] = ctraw

        xt_ready = {}
        xth_free = {}
        xt_read = []

        def prepare_a(b, bank):
            k = b % 2
            m = yield from layernorm(lambda t: X[:, b * TPB + t, :], tile_of(NRM), TPB, 0, [ld_x[b]],
                                     [nrm_read.get(0), *rows_read.get(0, [])])
            m = yield from layernorm(tile_of(NRM), tile_of(NRM), TPB, 0, [m], [])
            t = transposed(TPB, tile_of(NRM), [m], bank)
            nrm_read[0] = t
            d = dve([t, *xt_read, ct, *ld_g], lambda e: e.tensor_scalar(XT[:, 0:S], PSUM[:, bank, :], GAINS[:, 0:1],
                                                                        GAINS[:, 1:2], ALU.mult, ALU.add))
            d2 = dve([], lambda e: e.tensor_copy(XT[:, S:KEYS], CT[:, b * M:(b + 1) * M]))
            free[bank] = d
            yield
            xt_ready[b] = split_from(XT[:, :], XTH[:, k, :], XTL[:, k, :], [d2, xth_free.get(b - 2)])
            xt_read[:] = xt_ready[b]

        first = prepare_a(0, 7)
        for _ in range(6):
            next(first)

        wt = []
        WTB = [V[:, 1, 0, :], V[:, 1, 1, :]]
        for w, ld in ((0, ld_wq), (1, ld_wkv)):
            for half in range(2):
                bank = 2 * w + half
                m = transposed(4, lambda t, w=w, half=half: WA[:, w * INNER + (4 * half + t) * P:w * INNER + (4 * half + t + 1) * P],
                               [ld], bank)
                m = act([m], lambda e, w=w, half=half, bank=bank: e.activation(
                    WTB[w][:, half * 512:half * 512 + 512], PSUM[:, bank, :], ACT.Copy))
                free[bank] = m
                wt.append(m)
        finish(first)
        m_ready = {}
        for quad in range(H // 4):
            bank = 4 + quad % 2

            def prod(e, quad=quad, bank=bank):
                for j in range(4):
                    h = 8 * (quad // 2) + quad % 2 + 2 * j
                    r = slice(DH * (h % 2), DH * (h % 2) + DH)
                    c = slice((h // 2) * P, (h // 2 + 1) * P)
                    i = e.matmul(PSUM[:, bank, j * P:(j + 1) * P], WTB[0][r, c], WTB[1][r, c], start=True, stop=True)
                return i
            m = pe([*wt, free[bank]], prod)
            hs = slice(8 * (quad // 2) + quad % 2, 8 * (quad // 2) + 8, 2)
            hi, lo = MH[:, hs, :], ML[:, hs, :]
            src = PSUM[:, bank, :].rearrange("p (a b) -> p a b", a=4)
            a = act([m], lambda e, hi=hi, src=src: e.activation(hi, src, ACT.Copy, scale=DH ** -0.5))
            d = dve([a], lambda e, lo=lo, src=src, hi=hi: e.scalar_tensor_tensor(
                out=lo, in0=src, scalar=DH ** -0.5, in1=hi.bitcast(F32), op0=ALU.mult, op1=ALU.subtract))
            free[bank] = d
            m_ready[quad] = (a, d)
        wtb_read = m
        wvh, wvl = split_from(WA[:, 2 * INNER:3 * INNER], WVH[:, :], WVL[:, :], [ld_wkv])

        v_ready = {}
        pv_done = {}

        sets = [0]

        def next_set():
            sets[0] += 1
            return 2 * (sets[0] % 2)

        def values(b, kt):
            bank2 = next_set()
            k = b % 2
            cols = slice(kt * P, (kt + 1) * P)

            def issue(e):
                for n in range(2):
                    c = slice(n * BANK, (n + 1) * BANK)
                    i = three(e, PSUM[:, bank2 + n, :], XTH[:, k, cols], XTL[:, k, cols], WVH[:, c], WVL[:, c])
                return i
            m = pe([*xt_ready[b], wvh, wvl, free[bank2], free[bank2 + 1]], issue)
            a = act([m, pv_done.get((b - 2, PAIRS - 1)), wtb_read], lambda e: e.activation(
                V[:, k, kt, :].rearrange("p (a n) -> p a n", a=2), PSUM[:, bank2:bank2 + 2, :], ACT.Copy))
            free[bank2] = free[bank2 + 1] = a
            v_ready[b] = a

        def vctx(e):
            for n in range(2):
                c = slice(n * BANK, (n + 1) * BANK)
                i = three(e, PSUM[:, n, :], CTH[:, :], CTL[:, :], WVH[:, c], WVL[:, c])
            return i
        m = pe([cth, ctl, wvh, wvl, free[0], free[1]], vctx)
        vc_ready = act([m], lambda e: e.activation(VC[:, :].rearrange("p (a n) -> p a n", a=2), PSUM[:, 0:2, :], ACT.Copy))
        free[0] = free[1] = vc_ready
        for kt in range(KT):
            values(0, kt)

        a_ready = {}
        a_free = {}
        project_done = [None]

        def project(n):
            b, h = divmod(n, H)
            k, j = b % 2, n % 2
            m = pe([*xt_ready[b], *m_ready[2 * (h // 8) + h % 2], free[7]],
                   lambda e: three(e, PSUM[:, 7, :], MH[:, h, :], ML[:, h, :], XTH[:, k, 0:S], XTL[:, k, 0:S]))
            a = act([m, a_free.get(n - 2)], lambda e: e.activation(AH[:, j, :], PSUM[:, 7, :], ACT.Copy))
            d = dve([m, a], lambda e: e.tensor_tensor(AL[:, j, :], PSUM[:, 7, :], AH[:, j, :].bitcast(F32), ALU.subtract))
            free[7] = d
            a_ready[n] = (a, d)
            project_done[0] = m

        p_ready = {}
        p_read = {}
        exp_done = {}

        def scores(u):
            n, qt = divmod(u, TPB)
            b, h = divmod(n, H)
            k, j, r = b % 2, n % 2, u % 8
            bank = next_set()
            qs = slice(qt * P, (qt + 1) * P)

            def issue(e):
                for n2 in range(2):
                    ks = slice(n2 * HALF, (n2 + 1) * HALF)
                    i = three(e, PSUM[:, bank + n2, 0:HALF], AH[:, j, qs], AL[:, j, qs], XTH[:, k, ks], XTL[:, k, ks])
                return i
            m = pe([*a_ready[n], free[bank], free[bank + 1]], issue)
            if qt == TPB - 1:
                a_free[n] = m
                xth_free[b] = m
            sc = PSUM[:, bank:bank + 2, 0:HALF]
            d = dve([m], lambda e: e.tensor_reduce(NEGM[:, r:r + 1], sc, AX.XY, ALU.max, negate=True))
            a = act([d, p_read.get(u - 8)], lambda e: e.activation(
                PR[:, r, :].rearrange("p (a n) -> p a n", a=2), sc, ACT.Exp, bias=NEGM[:, r:r + 1],
                accum_out=ROWSUM[:, r:r + 1]))
            free[bank] = free[bank + 1] = exp_done[u] = a

        def normalise(u):
            r = u % 8
            d = dve([exp_done[u]], lambda e: e.reciprocal(RECIP[:, r:r + 1], ROWSUM[:, r:r + 1]))
            p_ready[u] = dve([d], lambda e: e.tensor_scalar(PR[:, r, :], PR[:, r, :], RECIP[:, r:r + 1], None, ALU.mult))

        pt_ready = {}

        def turn(u):
            n, qt = divmod(u, TPB)
            b, h = divmod(n, H)
            r, slot = u % 8, n % 4
            bank = 4 + u % 2

            def issue(e):
                for kt in range(KT):
                    i = e.transpose(PSUM[:, bank, kt * P:(kt + 1) * P], PR[:, r, kt * P:(kt + 1) * P], IDENT[:, :])
                return i
            m = pe([p_ready[u], free[bank]], issue)
            p_read[u] = m
            old = pv_done.get(divmod(n // 2 - 2, PAIRS)) if n // 2 >= 2 else None
            a = act([m, old], lambda e: e.activation(PT[:, slot, :, qt * P:(qt + 1) * P],
                                                     PSUM[:, bank, :].rearrange("p (k n) -> p k n", k=KT), ACT.Copy))
            free[bank] = a
            pt_ready[n] = [a]
            if qt == TPB - 1:
                def issue_c(e):
                    for t in range(TPB):
                        i = e.transpose(PSUM[0:M, 7, t * P:(t + 1) * P], PR[:, (n * TPB + t) % 8, S:KEYS], IDENT[:, :])
                    return i
                m = pe([free[7]], issue_c)
                for t in range(TPB):
                    p_read[n * TPB + t] = m
                c = dve([m, old], lambda e: e.tensor_copy(PTC[b * M:(b + 1) * M, slot, :], PSUM[0:M, 7, :]))
                free[7] = c
                pt_ready[n].append(c)

        ot_ready = {}
        ot_free = [None]

        def attend(pair, kt, part):
            qs = slice(part * S // 2, (part + 1) * S // 2)
            b, pr = divmod(pair, PAIRS)
            k = b % 2

            def issue(e):
                for j in range(2):
                    n = 2 * pair + j
                    h = n % H
                    dst = PSUM[DH * j:DH * j + DH, 6, qs]
                    if kt < KT:
                        i = e.matmul(dst, V[:, k, kt, h * DH:(h + 1) * DH], PT[:, n % 4, kt, qs], start=kt == 0, stop=False)
                    else:
                        i = e.matmul(dst, VC[b * M:(b + 1) * M, h * DH:(h + 1) * DH], PTC[b * M:(b + 1) * M, n % 4, qs],
                                     start=False, stop=True)
                return i
            waits = [*pt_ready[2 * pair], *pt_ready[2 * pair + 1], v_ready[b], vc_ready, free[6]] if (kt, part) == (0, 0) else []
            m = pe(waits, issue)
            if (kt, part) == (KT, 1):
                pv_done[(b, pr)] = m
                free[6] = dve([m, ot_free[0]], lambda e: e.tensor_copy(OT[:, pr, :], PSUM[:, 6, :]))
                ot_ready[pair] = free[6]

        x_ready = {}

        def add_to_x(b, m, bank):
            xb = X[:, b * TPB:(b + 1) * TPB, :]
            d = dve([m, x_ready.get(b)], lambda e: e.tensor_tensor(xb, xb, PSUM[:, bank, :].rearrange("p (t n) -> p t n", t=TPB),
                                                                   ALU.add))
            free[bank] = d
            x_ready[b] = d

        def project_out(b, src, weight, n, waits, bank):
            def issue(e):
                for t in range(TPB):
                    for c in range(n):
                        i = e.matmul(PSUM[:, bank, t * P:(t + 1) * P], src(c)[:, t * P:(t + 1) * P], weight(c),
                                     start=c == 0, stop=c == n - 1)
                return i
            m = pe([*waits, free[bank]], issue)
            add_to_x(b, m, bank)
            return m

        run_done = []
        slots_read = {}
        xf = XT[:, 0:S]

        pause = [0, 0]

        def normalised(b, nrm, xf, key, bank):
            m = yield from layernorm(lambda t: X[:, b * TPB + t, :], nrm, TPB, key % 4, [x_ready[b]],
                                     [nrm_read.get(key), *rows_read.get(key, [])])
            normed[b] = m
            for _ in range(pause[0]):
                yield
            t = transposed(TPB, nrm, [m], bank)
            nrm_read[key] = t
            if key < B:
                d = dve([t, *xf_read.get(key, [])], lambda e: e.tensor_copy(xf, PSUM[:, bank, :]))
            else:
                d = act([t, *xf_read.get(key, [])], lambda e: e.activation(xf, PSUM[:, bank, :], ACT.Copy))
            free[bank] = d
            yield
            return d

        def first_largest(vals, top, hot, tmp, tmp2, waits):
            m = dve(waits, lambda e: e.tensor_reduce(top, vals, AX.X, ALU.max))
            m = dve([m], lambda e: e.tensor_tensor(tmp, vals, top.unsqueeze(2).broadcast_to([P, TPB, E]), ALU.is_equal))
            yield
            m = dve([m, tie_ready], lambda e: e.tensor_tensor(tmp, tmp, TIE[:, :, :], ALU.mult))
            m = dve([m], lambda e: e.tensor_reduce(tmp2, tmp, AX.X, ALU.max))
            m = dve([m], lambda e: e.tensor_tensor(hot, tmp, tmp2.unsqueeze(2).broadcast_to([P, TPB, E]), ALU.is_equal))
            yield
            return m

        xf_read = {0: xt_read}
        listed = [{}, {}]
        s_rows = [[counter(f"rows_{w}{i}") for i in "01"] for w in "bd"]

        def over_e(v):
            return v.unsqueeze(2).broadcast_to([P, TPB, E])

        def route(b, which, bank, rows, rows2, xf, key):
            d = yield from normalised(b, tile_of(rows), xf, key, bank)
            if which == 1:
                copied = pool([normed[b], *rows_read.get(key, [])],
                              lambda e: e.tensor_copy(rows2[:, :, 0:D], rows[:, :, 0:D]))

            def issue(e):
                for t in range(TPB):
                    dst = PSUM[:, bank, t * E:(t + 1) * E]
                    i = e.matmul(dst, xf[:, t * P:(t + 1) * P], RW[:, which, :], start=True, stop=which == 1)
                    if which == 0:
                        i = e.matmul(dst, ONES[0:1, :], RB[0:1, :], start=False, stop=True)
                return i
            m = pe([d, ld_rw[which], ld_rb, ones_ready, free[bank]], issue)
            L, tmp, hot, hot2, L2, ex = (ROUT[:, b % 2, i] for i in range(6))
            top, top2, tmp2, sm, rc, rc2 = (RSM[:, b % 2, i] for i in range(6))
            lg = dve([m], lambda e: e.tensor_copy(L, PSUM[:, bank, 0:TPB * E].rearrange("p (t n) -> p t n", t=TPB)))
            free[bank] = lg
            xf_read[key] = xf_read.get(key, [])
            xf_read[key][:] = [m]
            yield
            m = yield from first_largest(L, top, hot, tmp, tmp2, [lg])
            hots = [hot]
            both = hot
            if which == 1:
                m = dve([m], lambda e: e.tensor_scalar(tmp, hot, -1.0, 1.0, ALU.mult, ALU.add))
                m = dve([m], lambda e: e.tensor_tensor(L2, L, tmp, ALU.mult))
                m = dve([m], lambda e: e.scalar_tensor_tensor(out=L2, in0=hot, scalar=-3.4e38, in1=L2, op0=ALU.mult,
                                                              op1=ALU.add))
                m = yield from first_largest(L2, top2, hot2, tmp, tmp2, [m])
                m = dve([m], lambda e: e.tensor_tensor(ex, hot, hot2, ALU.add))
                hots = [hot, hot2]
                both = ex

            for _ in range(pause[1]):
                yield
            def count(e):
                e.matmul(PSUM[:, bank, 0:TPB * E], LOWER[:, :], both, start=True, stop=True)
                return e.matmul(PSUM[:, bank, TPB * E:2 * TPB * E], ONES[:, :], both, start=True, stop=True)
            mc = pe([m, free[bank], lower_ready], count)
            if which == 0:
                m = dve([m], lambda e: e.tensor_tensor(L2, L, over_e(top), ALU.subtract))
                ae = act([m], lambda e: e.activation(ex, L2, ACT.Exp))
            else:
                m = dve([m], lambda e: e.tensor_tensor(tmp2, top2, top, ALU.subtract))
                ae = act([m], lambda e: e.activation(sm, tmp2, ACT.Exp))
            m = mc
            for t in range(TPB):
                at = b * TPB + t
                m = dve([m, run_ready, *run_done], lambda e, t=t, at=at: e.tensor_tensor(
                    RUN[:, which, at + 1, :], RUN[:, which, at, :], PSUM[:, bank, (TPB + t) * E:(TPB + t + 1) * E], ALU.add))
            run_done[:] = [m]
            place, share = PLACE[:, b % 2, 0], PLACE[:, b % 2, 1]
            p0 = dve([m], lambda e: e.tensor_tensor(place, RUN[:, which, b * TPB:(b + 1) * TPB, :],
                                                    PSUM[:, bank, 0:TPB * E].rearrange("p (t n) -> p t n", t=TPB), ALU.add))
            free[bank] = p0
            yield
            slots = []
            for k, h in enumerate(hots):
                m = dve([p0], lambda e, h=h: e.tensor_tensor(share, place, h, ALU.mult))
                m = dve([m], lambda e: e.tensor_reduce(RSM[:, b % 2, 6], share, AX.X, ALU.add))
                slots.append(dve([m, *slots_read.get(b % 2, [])], lambda e, k=k: e.tensor_copy(SLOT[:, b % 2, k, :], RSM[:, b % 2, 6])))
            if which == 0:
                m = dve([ae], lambda e: e.tensor_reduce(sm, ex, AX.X, ALU.add))
                m = dve([m], lambda e: e.reciprocal(rc, sm))
            else:
                m = dve([ae], lambda e: e.tensor_scalar(rc2, sm, 1.0, None, ALU.add))
                m = dve([m], lambda e: e.reciprocal(rc, rc2))
                m = dve([m], lambda e: e.tensor_tensor(rc2, sm, rc, ALU.mult))
            yield
            for k, (rr, c) in enumerate(((rows, rc), (rows2, rc2))[0:which + 1]):
                w = [m, jp_ready, *rows_read.get(key, [])]
                m1 = dve(w, lambda e, rr=rr, k=k: e.tensor_scalar(rr[:, :, D], JP[:, b * TPB:(b + 1) * TPB], float(k * N),
                                                                  None, ALU.add))
                m2 = dve(w, lambda e, rr=rr, c=c: e.tensor_copy(rr[:, :, D + 1], c))
                for t in range(TPB):
                    listed[which][b] = q.put(
                        "gpsimd", [slots[k], m1, m2, cleared[which], *([copied] if k else [])],
                        lambda e, rr=rr, t=t, k=k: e.indirect_dma_start(
                            LIST[which], bass.IndirectOffsetOnAxis(ap=SLOT[:, b % 2, k, t:t + 1].bitcast(U32), axis=0), rr[:, t, :], None),
                        s_rows[which][b % 2], 16)
            rows_read[key] = slots_read[b % 2] = [listed[which][b]]
            yield

        UNITS = B * H * TPB
        LAG = 3
        SHARE = [1, 2, 0, 0, 2, 2, 1, 2]
        pending = []

        def values_of(b):
            for kt in range(KT):
                values(b, kt)
                yield

        def out_of(b):
            ot_free[0] = project_out(b, lambda c: OT[:, c, :], lambda c: WOUT[:, c, :], PAIRS,
                                     [ot_ready[(b + 1) * PAIRS - 1], ld_wout], 7)

        project(0)
        project(1)
        for u in range(UNITS + LAG):
            if u < UNITS:
                n, qt = divmod(u, TPB)
                b, h = divmod(n, H)
                if qt == 0 and h == 3:
                    if b > 0:
                        background.append(route(b - 1, 0, 7, NRM, None, xf, 0))
                    if b + 1 < B:
                        background.append(prepare_a(b + 1, 7))
                        background.append(values_of(b + 1))
                scores(u)
            if 1 <= u <= UNITS:
                normalise(u - 1)
            for _ in range(min(len(pending), SHARE[u % 8])):
                attend(*pending.pop(0))
            if u < UNITS and qt == 1 and 1 <= n < B * H - 1:
                project(n + 1)
            advance()
            if u >= LAG:
                turn(u - LAG)
                if (u - LAG) % (2 * TPB) == 2 * TPB - 1:
                    pair = (u - LAG) // (2 * TPB)
                    while pending:
                        attend(*pending.pop(0))
                    if pair and pair % PAIRS == 0:
                        out_of(pair // PAIRS - 1)
                    pending = [(pair, kt, part) for part in range(2) for kt in range(KT + 1)]

        norm_buf = [PR[:, b, 0:TPB * ROW].rearrange("p (t n) -> p t n", t=TPB) for b in range(B)]
        norm_buf2 = [PR[:, B + b, 0:TPB * ROW].rearrange("p (t n) -> p t n", t=TPB) for b in range(B)]
        feat_buf = [OT[:, b, :] for b in range(B)]
        ring_free = {"x": {}, "y": {}}
        s_x = [counter(f"list_tile_{i}") for i in range(8)]
        s_y = [counter(f"result_rows_{i}") for i in range(4)]

        def tables(which, n_tiles, width):
            used, incl, shift = TAB[0:1, 0, :], TAB[0:1, 1, :], TAB[0:1, 2, :]
            has = HAS[0:1, :, :]
            pa, sh = PASSED[0:1, 0:n_tiles, :], SHIFT[0:1, 0:n_tiles, :]
            w = [lin_ready, incl_ready, jp_ready]
            m = dve(w, lambda e: e.tensor_tensor(has, RUN[0:1, which, NT, :].unsqueeze(2).broadcast_to([1, E, NT]),
                                                 LIN[0:1, :].rearrange("p (e t) -> p e t", e=E), ALU.is_gt))
            m = dve([m], lambda e: e.tensor_reduce(used, has, AX.X, ALU.add))
            m0 = dve([m], lambda e: e.tensor_tensor(TAB8[0:1, :, :], INCL[0:1, :, :],
                                                    used.unsqueeze(1).broadcast_to([1, E, E]), ALU.mult))
            m1 = dve([m], lambda e: e.tensor_scalar(shift, used, float(-P), float(N), ALU.mult, ALU.add))
            m = dve([m0], lambda e: e.tensor_reduce(incl, TAB8[0:1, :, :], AX.X, ALU.add))
            m = dve([m], lambda e: e.tensor_scalar(incl, incl, float(P), None, ALU.mult))
            m = dve([m], lambda e: e.tensor_tensor(pa, JP[0:1, 0:n_tiles].unsqueeze(2).broadcast_to([1, n_tiles, E]),
                                                   incl.unsqueeze(1).broadcast_to([1, n_tiles, E]), ALU.is_ge))
            m = dve([m, m1], lambda e: e.tensor_tensor(sh, pa, shift.unsqueeze(1).broadcast_to([1, n_tiles, E]), ALU.mult))
            r, c = LINROW[0:1, 0, 0:n_tiles], LINROW[0:1, 1, 0:n_tiles]
            m = dve([m], lambda e: e.tensor_reduce(r, sh, AX.X, ALU.add))
            ma = dve([m], lambda e: e.tensor_tensor(ROW_OF[0:1, 0:n_tiles], r, JP[0:1, 0:n_tiles], ALU.add))
            m = dve([m], lambda e: e.tensor_reduce(c, pa, AX.X, ALU.add))
            mb = dve([m], lambda e: e.tensor_scalar(W_OF[0:1, 0:n_tiles], c, float(E - 1), float(width), ALU.min, ALU.mult))
            mb = dve([m], lambda e: e.tensor_scalar(W2_OF[0:1, 0:n_tiles], c, float(E - 1), float(width // 2), ALU.min, ALU.mult))
            return ma, mb

        def experts(which, FF, n_tiles, weights1, weights2, ld1, ld2):
            NF = FF // P
            SETS = [0, 2] if FF == BANK else [0, 1, 2, 3]
            row_at, w_at = tables(which, n_tiles, 2 * FF)
            got, turned, gated, hid, hidt, idx_ready = ({} for _ in range(6))

            def fetch(j):
                r = j % 8

                def issue(e):
                    at = e.value_load(ROW_OF[0:1, j:j + 1], min_val=0, max_val=E * N + (n_tiles - 1) * P)
                    return e.dma_start(XG[:, r, :], LIST[which][bass.ds(at, P), :])
                got[j] = q.put("sync", [row_at, *listed[which].values(), ring_free["x"].get(r)], issue, s_x[r], 16)

            at1, at2 = {}, {}

            def read_columns(e, j1, j2):
                if j1 < n_tiles:
                    at1[j1] = e.value_load(W_OF[0:1, j1:j1 + 1], min_val=0, max_val=(E - 1) * 2 * FF)
                if j2 >= 0 and which == 1:
                    at2[j2] = at1[j2]
                elif j2 >= 0:
                    at2[j2] = e.value_load(W2_OF[0:1, j2:j2 + 1], min_val=0, max_val=(E - 1) * FF)

            def turn_x(j):
                r = j % 8
                def issue(e):
                    if j == 0:
                        read_columns(e, 0, -1)
                    return e.transpose(PSUM[:, 7, 0:P], XG[:, r, 0:D], IDENT[:, :])
                m = pe([got[j], free[7], w_at], issue)
                free[7] = turned[j] = dve([m, gated.get(j - 3)], lambda e: e.tensor_copy(XGT[:, j % 3, :], PSUM[:, 7, 0:P]))
                o = FILL[:, j % TPB:j % TPB + 1]
                m = dve([got[j], dump_ready], lambda e: e.tensor_scalar(o, XG[:, r, D:D + 1], 0.0, DUMP[:, j:j + 1], ALU.is_lt, ALU.mult))
                idx_ready[j] = dve([m, idx_free.get(r)], lambda e: e.tensor_tensor(IDX[:, r:r + 1], o, XG[:, r, D:D + 1], ALU.add))

            def gate_up(j):
                bank = SETS[j % len(SETS)]

                def issue(e):
                    for n in range(2 * FF // BANK):
                        i = e.matmul(PSUM[:, bank + n, :], XGT[:, j % 3, :], weights1[:, n * BANK:][:, bass.ds(at1[j], BANK)],
                                     start=True, stop=True)
                    read_columns(e, j + 1, j)
                    return i
                waits = [turned[j], w_at, free[bank], *ld1]
                if FF == BANK:
                    waits.append(free[bank + 1])
                m = gated[j] = pe(waits, issue)
                gate = PSUM[:, bank, 0:FF]
                up = PSUM[:, bank + 1, :] if FF == BANK else PSUM[:, bank, FF:2 * FF]
                sl = SIL[:, j % 3, 0:FF]
                a = act([m, hid_free.get(j % 3)], lambda e: e.activation(sl, gate, ACT.Silu))
                hid[j] = dve([a], lambda e: e.tensor_tensor(sl, sl, up, ALU.mult))
                free[bank] = hid[j]
                if FF == BANK:
                    free[bank + 1] = hid[j]

            def turn_h(j):
                bank = 4 + j % 2

                def issue(e):
                    for f in range(NF):
                        i = e.transpose(PSUM[:, bank, f * P:(f + 1) * P], SIL[:, j % 3, f * P:(f + 1) * P], IDENT[:, :])
                    return i
                m = hid_free[j % 3] = pe([hid[j], free[bank]], issue)
                hidt[j] = free[bank] = act([m, hidt_free.get(j % 2), ot_free[0]], lambda e: e.activation(
                    HIDT[:, j % 2, 0:FF], PSUM[:, bank, 0:FF], ACT.Copy))

            def down(j):
                r = j % 8

                def issue(e):
                    for f in range(NF):
                        i = e.matmul(PSUM[:, 6, 0:D], HIDT[:, j % 2, f * P:(f + 1) * P],
                                     weights2[:, f * D:][:, bass.ds(at2[j], D)], start=f == 0, stop=f == NF - 1)
                    return i
                m = hidt_free[j % 2] = pe([hidt[j], free[6], *ld2], issue)
                y = dve([m, ring_free["y"].get(j % 4)], lambda e: e.tensor_scalar(
                    YS[:, j % 4, :], PSUM[:, 6, 0:D], XG[:, r, D + 1:D + 2], None, ALU.mult))
                free[6] = ring_free["x"][r] = y
                idx_free[r] = ring_free["y"][j % 4] = q.put(
                    "gpsimd", [y, idx_ready[j]], lambda e: e.indirect_dma_start(
                        RES[which], bass.IndirectOffsetOnAxis(ap=IDX[:, r:r + 1].bitcast(U32), axis=0), YS[:, j % 4, :], None),
                    s_y[j % 4], 16)
                return m

            dump_ready = dve([jp_ready], lambda e: e.tensor_scalar(DUMP[:, 0:n_tiles], JP[:, 0:n_tiles],
                                                          float((which + 1) * N + 1), None, ALU.add))
            for j in range(8):
                fetch(j)
            turn_x(0)
            turn_x(1)
            for j in range(n_tiles + 2):
                if j < n_tiles:
                    gate_up(j)
                if j + 2 < n_tiles:
                    turn_x(j + 2)
                if j >= 2:
                    last = down(j - 2)
                    if j + 6 < n_tiles:
                        fetch(j + 6)
                if 1 <= j <= n_tiles:
                    turn_h(j - 1)
            landed = [*[ring_free["y"][i] for i in range(4)], kb_ready[B - 1], vb_ready[B - 1]]
            for k in range(which + 1):
                for b in range(B):
                    c = counter(f"back_{which}_{k}_{b}")
                    dst = PT[:, 2 * k, b, :].rearrange("p (t n) -> p t n", t=TPB)
                    src = RES[which][k * N + b * S:k * N + (b + 1) * S, :].rearrange("(t p) n -> p t n", p=P)
                    back[(which, k, b)] = (q.put("sync", landed, lambda e, dst=dst, src=src: e.dma_start(dst, src), c, 16), dst)
            return last

        def take_back(which, b):
            xb = X[:, b * TPB:(b + 1) * TPB, :]
            for k in range(which + 1):
                m, y = back[(which, k, b)]
                x_ready[b] = dve([m, x_ready[b]], lambda e, y=y: e.tensor_tensor(xb, xb, y, ALU.add))

        back, hid_free, hidt_free, idx_free = {}, {}, {}, {}

        ld_w1.append(load("w1b", W1ALL[:, 4 * 2 * F_B:].rearrange("p (e n) -> p e n", e=E - 4),
                          w1[4:].rearrange("e p n -> p e n"), [pv_done[(B - 2, PAIRS - 1)]]))
        while pending:
            attend(*pending.pop(0))
        out_of(B - 1)
        finish(route(B - 1, 0, 7, NRM, None, xf, 0))
        ld_w2 = [load(f"w2_{c}", W2ALL.rearrange("p (e c n) -> p c e n", e=E, c=F_B // P)[:, c],
                      w2.rearrange("e (c p) n -> c p e n", p=P)[c], [pv_done[(B - 1, PAIRS - 1)]]) for c in range(F_B // P)]

        pv_last = pv_done[(B - 1, PAIRS - 1)]
        p1 = pool([pv_last], lambda e: e.memset(MASK1[:, :, :], 1.0))
        p2 = pool([], lambda e: e.memset(MASK2[:, :, :], 1.0))
        p4 = pool([p2], lambda e: e.affine_select(out=MASK1[:, :, :], in_=MASK1[:, :, :], compare_op=ALU.is_ge, fill=0.0,
                                                  base=0, pattern=[[-DC, HC], [0, M]], channel_multiplier=1))
        p5 = pool([p4], lambda e: e.affine_select(out=MASK1[:, :, :], in_=MASK1[:, :, :], compare_op=ALU.is_ge, fill=0.0,
                                                  base=DC - 1, pattern=[[DC, HC], [0, M]], channel_multiplier=-1))
        p6 = pool([p4], lambda e: e.affine_select(out=MASK2[:, :, :], in_=MASK2[:, :, :], compare_op=ALU.is_ge, fill=0.0,
                                                  base=0, pattern=[[P, 4], [-M, HC]], channel_multiplier=1))
        masks_ready = pool([p6], lambda e: e.affine_select(out=MASK2[:, :, :], in_=MASK2[:, :, :], compare_op=ALU.is_ge,
                                                           fill=0.0, base=M - 1, pattern=[[-P, 4], [M, HC]],
                                                           channel_multiplier=-1))

        WKREP = WC[:, 3, :]
        m = dve([ld_ckv], lambda e: e.tensor_copy(WKREP.rearrange("p (h d) -> p h d", h=HC),
                                                  WC[:, 2, 0:DC].unsqueeze(1).broadcast_to([P, HC, DC])))
        m2 = dve([ctraw, pv_last], lambda e: e.tensor_copy(
            CTREP[:, :, :, :], CTRAW[:, :].rearrange("p (b k) -> p b k", b=B).unsqueeze(2).broadcast_to([P, B, 4, M])))
        mk = pe([m2, free[0]], lambda e: e.matmul(PSUM[:, 0, 0:P], WKREP, CTRAW[:, :], start=True, stop=True))
        kr = dve([mk], lambda e: e.tensor_copy(KREP[:, :], PSUM[:, 0, 0:P]))
        free[0] = kr

        def vrep(e):
            for b in range(B):
                i = e.matmul(PSUM[:, 1, b * DC:(b + 1) * DC], CTREP[:, b, :, :], WC[:, 2, DC:2 * DC], start=True, stop=True)
            return i
        mv = pe([free[1]], vrep)
        vr = dve([mv], lambda e: e.tensor_copy(VREP[:, :, :], PSUM[:, 1, 0:B * DC].rearrange("p (b d) -> p b d", b=B)))
        free[1] = vr
        kb_ready, vb_ready = {}, {}
        for b in range(B):
            kb_ready[b] = pool([kr, masks_ready], lambda e, b=b: e.tensor_tensor(
                KB[:, b, :, :], MASK1[:, :, :], KREP[:, b * M:(b + 1) * M].unsqueeze(1).broadcast_to([P, HC, M]), ALU.mult))
            vb_ready[b] = pool([vr, masks_ready], lambda e, b=b: e.tensor_tensor(
                VB[:, b, :, :].rearrange("p c (h d) -> p (c h) d", h=HC),
                MASK2[:, :, :].rearrange("p c h -> p (c h)").unsqueeze(2).broadcast_to([P, 4 * HC, DC]),
                VREP[:, b, :].unsqueeze(1).broadcast_to([P, 4 * HC, DC]), ALU.mult))


        last_b = experts(0, F_B, TILES_B, W1ALL, W2ALL, ld_w1, ld_w2)

        ld_d1 = [load(f"wgu{i}", WGUALL.rearrange("p (e a n) -> p a e n", e=E, a=2)[:, i], w.rearrange("e p n -> p e n"), [last_b])
                 for i, w in enumerate((Wg, Wu))]
        ld_d2 = [load(f"wd_{c}", WDALL.rearrange("p (e c n) -> p c e n", e=E, n=P)[:, c],
                      Wd.rearrange("e (c p) n -> c p e n", p=P)[c], [last_b]) for c in range(F_D // P)]
        QT = [PR[:, b, 0:S] for b in range(B)]
        OC = OT[:, 4:6, :]
        q_ready, q_read, oc_free, pc_free, ptc_free = {}, {}, {}, {}, {}

        def prepare_c(b):
            take_back(0, b)
            d = yield from normalised(b, tile_of(norm_buf[b]), feat_buf[b], b + 4, 4 + b)
            m = pe([d, ld_cq, free[b]], lambda e: e.matmul(PSUM[:, b, :], WC[:, 0, :], feat_buf[b], start=True, stop=True))
            xf_read[b + 4] = [m]
            q_ready[b] = act([m], lambda e: e.activation(QT[b], PSUM[:, b, :], ACT.Copy))
            free[b] = q_ready[b]
            yield

        def over_k(v):
            return v.unsqueeze(2).broadcast_to([P, HC, M])

        def heads_of(v):
            return v.rearrange("p (h k) -> p h k", h=HC)

        c_exp, c_norm, c_turned = {}, {}, {}

        def scores_c(i):
            b, t = divmod(i, TPB)
            bank, r = i % 4, i % 4
            m = pe([q_ready[b], kb_ready[b], free[bank]], lambda e: e.matmul(
                PSUM[:, bank, :], QT[b][:, t * P:(t + 1) * P], KB[:, b, :, :], start=True, stop=True))
            q_read[b] = m
            top, pc = CSTAT[:, r, 0, :], PT[:, 2, r, :]
            d = dve([m], lambda e: e.tensor_reduce(top, heads_of(PSUM[:, bank, :]), AX.X, ALU.max))
            d = dve([d, pc_free.get(r)], lambda e: e.tensor_tensor(heads_of(pc), heads_of(PSUM[:, bank, :]), over_k(top),
                                                                   ALU.subtract))
            free[bank] = d
            c_exp[i] = act([d], lambda e: e.activation(pc, pc, ACT.Exp, scale=DC ** -0.5))

        def normalise_c(i):
            r = i % 4
            sm, rc, pc = CSTAT[:, r, 1, :], CSTAT[:, r, 2, :], PT[:, 2, r, :]
            d = dve([c_exp[i]], lambda e: e.tensor_reduce(sm, heads_of(pc), AX.X, ALU.add))
            d = dve([d], lambda e: e.reciprocal(rc, sm))
            c_norm[i] = pool([d], lambda e: e.tensor_tensor(heads_of(pc), heads_of(pc), over_k(rc), ALU.mult))

        def turn_c(i):
            b, t = divmod(i, TPB)
            k, r, bank = b % 2, i % 4, 4 + i % 2
            pc = PT[:, 2, r, :]

            def issue(e):
                for c in range(4):
                    j = e.transpose(PSUM[:, bank, c * P:(c + 1) * P], pc[:, c * P:(c + 1) * P], IDENT[:, :])
                return j
            m = pe([c_norm[i], free[bank]], issue)
            pc_free[r] = m
            a = act([m, ptc_free.get(b - 2)], lambda e: e.activation(
                PT[:, k, :, t * P:(t + 1) * P], PSUM[:, bank, :].rearrange("p (c n) -> p c n", c=4), ACT.Copy))
            free[bank] = a
            c_turned[b] = a

        def out_c(b):
            k = b % 2

            def issue(e):
                for c in range(4):
                    i = e.matmul(PSUM[:, 6, :], VB[:, b, c, :], PT[:, k, c, :], start=c == 0, stop=c == 3)
                return i
            m = pe([c_turned[b], vb_ready[b], free[6]], issue)
            ptc_free[b] = m
            o = dve([m, oc_free.get(b - 2)], lambda e: e.tensor_copy(OC[:, k, :], PSUM[:, 6, :]))
            free[6] = o
            yield
            oc_free[b] = project_out(b, lambda c: OC[:, k, :], lambda c: WC[:, 1, :], 1, [o, ld_cc], 6)
            yield
            yield from route(b, 1, 7, norm_buf[b], norm_buf2[b], feat_buf[b], b + 4)

        LAG_C = 2
        pause[:] = [3, 3]
        for b in range(B):
            background.append(prepare_c(b))
            advance(1, B)
        while len(background) > 2:
            advance(1, B)
        for i in range(NT + LAG_C):
            if i < NT:
                scores_c(i)
            if 1 <= i <= NT:
                normalise_c(i - 1)
            advance(3, 2)
            if i >= LAG_C:
                turn_c(i - LAG_C)
                if (i - LAG_C) % TPB == TPB - 1:
                    background.append(out_c((i - LAG_C) // TPB))
        while background:
            advance(1, 2)

        experts(1, F_D, TILES_D, WGUALL, WDALL, ld_d1, ld_d2)
        for b in range(B):
            take_back(1, b)

        s_out = counter("stored")
        for b in range(B):
            stored = q.put("sync", [x_ready[b]], lambda e, b=b: e.dma_start(
                out_v[:, b * TPB:(b + 1) * TPB, :], X[:, b * TPB:(b + 1) * TPB, :]), s_out, 16)
        q.wait("sync", [stored])

        with nc.Block() as block:
            @block.sync
            def _(eng):
                q.emit("sync", eng)

            @block.gpsimd
            def _(eng):
                q.emit("gpsimd", eng)

            @block.scalar
            def _(eng):
                q.emit("scalar", eng)

            @block.vector
            def _(eng):
                q.emit("vector", eng)

            @block.tensor
            def _(eng):
                q.emit("tensor", eng)


_INS = ['x', 'ctx_1024', 'L0_xattn_ln_m_g', 'L0_xattn_ln_m_b', 'L0_xattn_ln_l_g', 'L0_xattn_ln_l_b', 'L0_xattn_Wq',
        'L0_xattn_Wkv', 'L0_xattn_Wout', 'L0_ffn_router_w', 'L0_ffn_router_b', 'L0_ffn_w1', 'L0_ffn_w2', 'L1_xattn_w_q',
        'L1_xattn_w_kv', 'L1_xattn_w_concat', 'L1_ffn_Wr', 'L1_ffn_Wg', 'L1_ffn_Wu', 'L1_ffn_Wd']


def kernel(**inputs):
    import numpy as _np
    import concourse.bacc as _bacc
    from concourse import mybir as _mybir
    from concourse.bass_utils import run_bass_kernel_spmd as _run

    nc = _bacc.Bacc("TRN2", target_bir_lowering=False, num_devices=1)
    arrays, args = {}, []
    for name in _INS:
        a = _np.ascontiguousarray(inputs[name])
        arrays[f"in_{name}"] = a
        args.append(nc.dram_tensor(f"in_{name}", a.shape, _mybir.dt.from_np(a.dtype), kind="ExternalInput").ap())
    shape = _np.shape(inputs["x"])
    args.append(nc.dram_tensor("out_x", shape, _mybir.dt.float32, kind="ExternalOutput").ap())
    build(nc, *args)
    return _run(nc, [arrays], core_ids=[0]).results[0]["out_x"]
```
